# Optimizing a Trainium2 kernel written in Bass

```python
import numpy as np
import jax
import jax.numpy as jnp

def _softmax(x, axis=-1):
    return jax.nn.softmax(x, axis=axis)

def _gelu(x):
    return jax.nn.gelu(x, approximate=True)

def _silu(x):
    return jax.nn.silu(x)

def _sigmoid(x):
    return jax.nn.sigmoid(x)

def _layernorm(x, axis=-1, eps=1e-05):
    m = jnp.mean(x, axis=axis, keepdims=True)
    v = jnp.var(x, axis=axis, keepdims=True)
    return (x - m) / jnp.sqrt(v + eps)

def _scatter_add(tgt, idx, src, axis=0):
    return tgt.at[idx].add(src)

def _segment_sum(src, seg, n):
    return jax.ops.segment_sum(src, seg, n)
kernel_name = 'mk_seq_postln_d1_jaxref_r2_f7d420'

def setup_inputs(seed: int=0):
    np.random.seed(seed)
    _w = jnp.asarray

    def _L0_attn_setup():
        import jax, jax.numpy as jnp
        import numpy as np
        DIM = 512
        NUM_HEAD = 16
        DIM_HEAD = DIM // NUM_HEAD
        RMS_EPS = 1.1920929e-07
        EPS_LIN = 1e-06
        THETA = 10000.0

        def rmsnorm(x, g, eps=RMS_EPS):
            return x * jax.lax.rsqrt(jnp.mean(x * x, axis=-1, keepdims=True) + eps) * g

        def rope_cos_sin(seq_len, dim_head, dtype=jnp.float32):
            inv_freq = 1.0 / THETA ** (jnp.arange(0, dim_head, 2, dtype=dtype) / dim_head)
            t = jnp.arange(seq_len, dtype=dtype)
            freqs = jnp.outer(t, inv_freq)
            return (jnp.cos(freqs), jnp.sin(freqs))

        def apply_rope(t, cos, sin):
            tr = t[..., 0::2]
            ti = t[..., 1::2]
            out_r = tr * cos - ti * sin
            out_i = tr * sin + ti * cos
            return jnp.stack([out_r, out_i], axis=-1).reshape(t.shape)
        key = jax.random.key(seed)
        ks = jax.random.split(key, 5)
        B, L = (4, 2048)
        x = jax.random.normal(ks[0], (B, L, DIM), dtype=jnp.float32)
        Wqkv = jax.random.normal(ks[1], (3 * DIM, DIM), dtype=jnp.float32) * 0.02
        bqkv = jax.random.normal(ks[2], (3 * DIM,), dtype=jnp.float32) * 0.02
        gq = jnp.ones((DIM,), dtype=jnp.float32)
        gk = jnp.ones((DIM,), dtype=jnp.float32)
        Wout = jax.random.normal(ks[3], (DIM, DIM), dtype=jnp.float32) * 0.02
        bout = jax.random.normal(ks[4], (DIM,), dtype=jnp.float32) * 0.02
        gout = jnp.ones((DIM,), dtype=jnp.float32)
        return {'x': x, 'Wqkv': Wqkv, 'bqkv': bqkv, 'gq': gq, 'gk': gk, 'Wout': Wout, 'bout': bout, 'gout': gout}
    _L0_attn_in = _L0_attn_setup()

    def _L0_ffn_setup():
        import jax, jax.numpy as jnp
        import numpy as np
        DIM = 512

        def _reference_tuple_inner(x, W_r, W_k, W_v, mu_r, mu_k):
            B, T, C = x.shape
            x_prev = jnp.concatenate([jnp.zeros((B, 1, C), x.dtype), x[:, :-1, :]], axis=1)
            xr = mu_r * x + (1.0 - mu_r) * x_prev
            xk = mu_k * x + (1.0 - mu_k) * x_prev
            r = jax.nn.sigmoid(jnp.einsum('btc,dc->btd', xr, W_r))
            k = jnp.einsum('btc,dc->btd', xk, W_k)
            k_act = jnp.square(jax.nn.relu(k))
            out = r * jnp.einsum('btc,dc->btd', k_act, W_v)
            new_state = x[:, -1, :]
            return (out, new_state)
        key = jax.random.key(seed)
        ks = jax.random.split(key, 6)
        B, T, C = (8, 1024, DIM)
        x = jax.random.normal(ks[0], (B, T, C), dtype=jnp.float32)
        s = 1.0 / np.sqrt(C)
        W_r = jax.random.uniform(ks[1], (C, C), jnp.float32, -s, s)
        W_k = jax.random.uniform(ks[2], (C, C), jnp.float32, -s, s)
        W_v = jax.random.uniform(ks[3], (C, C), jnp.float32, -s, s)
        mu_r = jax.random.uniform(ks[4], (C,), jnp.float32)
        mu_k = jax.random.uniform(ks[5], (C,), jnp.float32)
        return {'x': x, 'W_r': W_r, 'W_k': W_k, 'W_v': W_v, 'mu_r': mu_r, 'mu_k': mu_k}
    _L0_ffn_in = _L0_ffn_setup()
    _d = {'L0_attn_x': _L0_attn_in['x'], 'L0_attn_Wqkv': _L0_attn_in['Wqkv'], 'L0_attn_bqkv': _L0_attn_in['bqkv'], 'L0_attn_gq': _L0_attn_in['gq'], 'L0_attn_gk': _L0_attn_in['gk'], 'L0_attn_Wout': _L0_attn_in['Wout'], 'L0_attn_bout': _L0_attn_in['bout'], 'L0_attn_gout': _L0_attn_in['gout'], 'L0_ffn_W_r': _L0_ffn_in['W_r'], 'L0_ffn_W_k': _L0_ffn_in['W_k'], 'L0_ffn_W_v': _L0_ffn_in['W_v'], 'L0_ffn_mu_r': _L0_ffn_in['mu_r'], 'L0_ffn_mu_k': _L0_ffn_in['mu_k']}
    _x0 = _d['L0_attn_x']
    _d['L0_attn_x'] = jax.random.normal(jax.random.fold_in(jax.random.key(seed), 1), (16, 1024, 512), dtype=_x0.dtype)
    del _x0
    return _d

def reference(L0_attn_x, L0_attn_Wqkv, L0_attn_bqkv, L0_attn_gq, L0_attn_gk, L0_attn_Wout, L0_attn_bout, L0_attn_gout, L0_ffn_W_r, L0_ffn_W_k, L0_ffn_W_v, L0_ffn_mu_r, L0_ffn_mu_k):

    def _L0_attn_ref(x, Wqkv, bqkv, gq, gk, Wout, bout, gout):
        import jax, jax.numpy as jnp
        import numpy as np
        DIM = 512
        NUM_HEAD = 16
        DIM_HEAD = DIM // NUM_HEAD
        RMS_EPS = 1.1920929e-07
        EPS_LIN = 1e-06
        THETA = 10000.0

        def rmsnorm(x, g, eps=RMS_EPS):
            return x * jax.lax.rsqrt(jnp.mean(x * x, axis=-1, keepdims=True) + eps) * g

        def rope_cos_sin(seq_len, dim_head, dtype=jnp.float32):
            inv_freq = 1.0 / THETA ** (jnp.arange(0, dim_head, 2, dtype=dtype) / dim_head)
            t = jnp.arange(seq_len, dtype=dtype)
            freqs = jnp.outer(t, inv_freq)
            return (jnp.cos(freqs), jnp.sin(freqs))

        def apply_rope(t, cos, sin):
            tr = t[..., 0::2]
            ti = t[..., 1::2]
            out_r = tr * cos - ti * sin
            out_i = tr * sin + ti * cos
            return jnp.stack([out_r, out_i], axis=-1).reshape(t.shape)
        B, L, D = x.shape
        qkv = x @ Wqkv.T + bqkv
        q, k, v = jnp.split(qkv, 3, axis=-1)
        q = rmsnorm(q, gq)
        k = rmsnorm(k, gk)
        split = lambda t: t.reshape(B, L, NUM_HEAD, DIM_HEAD).transpose(0, 2, 1, 3)
        q, k, v = (split(q), split(k), split(v))
        cos, sin = rope_cos_sin(L, DIM_HEAD)
        cos = cos[None, None]
        sin = sin[None, None]
        q = apply_rope(q, cos, sin)
        k = apply_rope(k, cos, sin)
        qf = jax.nn.relu(q)
        kf = jax.nn.relu(k)
        vpad = jnp.concatenate([v, jnp.ones_like(v[..., :1])], axis=-1)
        vk = jnp.einsum('bhlp,bhld->bhpd', vpad, kf)
        res = jnp.einsum('bhpd,bhld->bhlp', vk, qf)
        attn = res[..., :-1] / (res[..., -1:] + EPS_LIN)
        attn = attn.transpose(0, 2, 1, 3).reshape(B, L, D)
        out = rmsnorm(attn @ Wout.T + bout, gout)
        return out

    def _L0_ffn_ref(x, W_r, W_k, W_v, mu_r, mu_k):
        import jax, jax.numpy as jnp
        import numpy as np
        DIM = 512

        def _reference_tuple_inner(x, W_r, W_k, W_v, mu_r, mu_k):
            B, T, C = x.shape
            x_prev = jnp.concatenate([jnp.zeros((B, 1, C), x.dtype), x[:, :-1, :]], axis=1)
            xr = mu_r * x + (1.0 - mu_r) * x_prev
            xk = mu_k * x + (1.0 - mu_k) * x_prev
            r = jax.nn.sigmoid(jnp.einsum('btc,dc->btd', xr, W_r))
            k = jnp.einsum('btc,dc->btd', xk, W_k)
            k_act = jnp.square(jax.nn.relu(k))
            out = r * jnp.einsum('btc,dc->btd', k_act, W_v)
            new_state = x[:, -1, :]
            return (out, new_state)
        return _reference_tuple_inner(x, W_r, W_k, W_v, mu_r, mu_k)[0]
    x = L0_attn_x
    x = _layernorm(x + _L0_attn_ref(x, L0_attn_Wqkv, L0_attn_bqkv, L0_attn_gq, L0_attn_gk, L0_attn_Wout, L0_attn_bout, L0_attn_gout), axis=-1)
    x = _layernorm(x + _L0_ffn_ref(x, L0_ffn_W_r, L0_ffn_W_k, L0_ffn_W_v, L0_ffn_mu_r, L0_ffn_mu_k), axis=-1)
    return x

_drawn_inputs = setup_inputs


def setup_inputs(seed=0):
    import zlib

    import numpy as np

    out = dict(_drawn_inputs(seed))
    spreads = {'L0_attn_gq': (1.0, 0.6), 'L0_attn_gk': (1.0, 0.6), 'L0_attn_gout': (1.0, 0.2)}
    factors = {'L0_ffn_mu_r': 7.822}
    for name, (base, spread) in spreads.items():
        noise = np.random.default_rng([zlib.crc32(name.encode()), seed]).standard_normal(out[name].shape)
        drawn = base * np.exp(spread * noise) if base else spread * noise
        out[name] = jnp.asarray(drawn.astype(out[name].dtype))
    for name, factor in factors.items():
        out[name] = (out[name] * factor).astype(out[name].dtype)
    return out
```

```python
from contextlib import ExitStack

import numpy as np

import concourse.bass as bass
from concourse import mybir

ALU = mybir.AluOpType
ACT = mybir.ActivationFunctionType
F32 = mybir.dt.float32
F32R = mybir.dt.float32r

P = 128
HEADS = 16
RMS_EPS = 1.1920929e-07
EPS_LIN = 1e-06
LN_EPS = 1e-05


def need(eng, sem, count):
    if not isinstance(count, int) or count > 0:
        eng.wait_ge(sem, count)


def f32(ap):
    return ap.bitcast(F32)


def postnorm_layer(nc, x, w_qkv, b_qkv, g_qk, w_out, b_out, g_out, w_r, w_k, w_v, mu_r, mu_k,
                   rope_cos, rope_sin, identity, out, y_mid):
    TOKENS, D = x.shape
    L = rope_cos.shape[0]
    KC = D // P
    DH = D // HEADS
    HF = DH // 2
    HC = P // DH
    NC = HEADS // HC
    EW = DH + 1
    TILES = TOKENS // P
    TB = L // P
    assert TB % 2 == 0 and TILES % TB == 0
    BT = 4
    BLK = BT * P
    BLOCKS = TOKENS // BLK
    BPB = L // BLK
    assert BPB == 2

    ctx = ExitStack()

    def sb(scope, name, shape, dt=F32):
        return scope.enter_context(nc.sbuf_tensor(name, shape, dt))

    def sem(name):
        return ctx.enter_context(nc.semaphore(name))

    with ctx:
        WR, WKF, WVF = range(3)
        wb_hi = sb(ctx, "wb_hi", [P, 3, KC, D], F32R)
        wb_lo = sb(ctx, "wb_lo", [P, 3, KC, D], F32R)
        ln_eps = sb(ctx, "ln_eps", [P, 1])
        ident = sb(ctx, "ident", [P, P])
        mu = sb(ctx, "mu", [P, 2, KC])
        w_pieces = [w_qkv[:, 0:D], w_qkv[:, D:2 * D], w_qkv[:, 2 * D:3 * D], w_out, w_r, w_k, w_v]

        weight_in = [sem("weight_in0"), sem("weight_in1")]
        const_in = sem("const_in")
        weight_hi = sem("weight_hi")
        weight_done = sem("weight_done")

        with ExitStack() as pa:
            WQ, WK, WV, WO = range(4)
            wa_hi = sb(pa, "wa_hi", [P, 4, KC, D], F32R)
            wa_lo = sb(pa, "wa_lo", [P, 4, KC, D], F32R)
            split = [(wa_hi[:, w], wa_lo[:, w]) for w in range(4)] + [(wb_hi[:, w], wb_lo[:, w]) for w in range(3)]
            rms_eps = sb(pa, "rms_eps", [P, 1])
            psum_q = pa.enter_context(nc.psum_tensor("psum_q", [P, D], F32))
            psum_k = pa.enter_context(nc.psum_tensor("psum_k", [P, D], F32))
            psum_v = pa.enter_context(nc.psum_tensor("psum_v", [P, D], F32))
            psum_o = pa.enter_context(nc.psum_tensor("psum_o", [P, D], F32))
            psum_t = pa.enter_context(nc.psum_tensor("psum_t", [P, D], F32))
            psum_kv = pa.enter_context(nc.psum_tensor("psum_kv", [P, D], F32))
            psum_n = pa.enter_context(nc.psum_tensor("psum_n", [P, 2, D], F32))
            kv_cols = psum_kv[:, 0:NC * EW].rearrange("p (c e) -> p c e", e=EW)

            bias_qkv = sb(pa, "bias_qkv", [P, 3 * D])
            gain_qk = sb(pa, "gain_qk", [P, 2 * D])
            bias_o = sb(pa, "bias_o", [P, D])
            gain_o = sb(pa, "gain_o", [P, D])
            cos_t = sb(pa, "cos_t", [P, TB, HF])
            sin_t = sb(pa, "sin_t", [P, TB, DH])
            ones = sb(pa, "ones", [P, HEADS])
            x_in = sb(pa, "x_in", [P, 2, D])
            x_res = sb(pa, "x_res", [P, 2, D])
            xT_hi = sb(pa, "xT_hi", [P, 2, KC, P], F32R)
            xT_lo = sb(pa, "xT_lo", [P, 2, KC, P], F32R)
            q_raw = sb(pa, "q_raw", [P, D])
            k_raw = sb(pa, "k_raw", [P, D])
            v_raw = sb(pa, "v_raw", [P, D])
            q_g = sb(pa, "q_g", [P, D])
            k_g = sb(pa, "k_g", [P, D])
            q_cos = sb(pa, "q_cos", [P, D])
            q_sin = sb(pa, "q_sin", [P, D])
            k_cos = sb(pa, "k_cos", [P, D])
            k_sin = sb(pa, "k_sin", [P, D])
            q_ring = sb(pa, "q_ring", [P, TB, D])
            q_tile = sb(pa, "q_tile", [P, 2, D])
            k_rot = sb(pa, "k_rot", [P, D])
            k_feat = sb(pa, "k_feat", [P, D])
            v_ext = sb(pa, "v_ext", [P, HEADS, EW])
            squares = sb(pa, "squares", [P, D])
            sum_sq = sb(pa, "sum_sq", [P, 4])
            rms_qk = sb(pa, "rms_qk", [P, 2])
            inv_rms_k = sb(pa, "inv_rms_k", [P, 1])
            eps_q = sb(pa, "eps_q", [P, TB])
            qT_hi = sb(pa, "qT_hi", [P, NC, P], F32R)
            qT_lo = sb(pa, "qT_lo", [P, NC, P], F32R)
            kv_hi = sb(pa, "kv_hi", [P, NC, HC, EW], F32R)
            kv_lo = sb(pa, "kv_lo", [P, NC, HC, EW], F32R)
            den = sb(pa, "den", [P, 2, HEADS])
            attn = sb(pa, "attn", [P, D])
            aT_hi = sb(pa, "aT_hi", [P, KC, P], F32R)
            aT_lo = sb(pa, "aT_lo", [P, KC, P], F32R)
            o_raw = sb(pa, "o_raw", [P, D])
            o_norm = sb(pa, "o_norm", [P, D])
            h_sum = sb(pa, "h_sum", [P, D])
            inv_rms_o = sb(pa, "inv_rms_o", [P, 1])
            stats = sb(pa, "stats", [P, 6])
            mean_var = sb(pa, "mean_var", [P, 2])
            std_h = sb(pa, "std_h", [P, 1])
            inv_std = sb(pa, "inv_std", [P, 1])
            y_out = sb(pa, "y_out", [P, 2, D])
            w_stage = q_ring[:, :, :].rearrange("p (s c) d -> p s c d", s=2)

            x_loaded = [sem("x_loaded0"), sem("x_loaded1")]
            res_loaded = [sem("res_loaded0"), sem("res_loaded1")]
            q_fetched = [sem("q_fetched0"), sem("q_fetched1")]
            y_stored = [sem("y_stored0"), sem("y_stored1")]
            consts_set = sem("consts_set")
            t_x = sem("t_x")
            t_v = sem("t_v")
            t_a = sem("t_a")
            t_q = sem("t_q")
            t_o = sem("t_o")
            t_qT = sem("t_qT")
            t_kv = sem("t_kv")
            t_k = sem("t_k")
            t_n = sem("t_n")
            a_x = sem("a_x")
            a_v = sem("a_v")
            a_kf = sem("a_kf")
            a_a = sem("a_a")
            a_sq = sem("a_sq")
            a_qT = sem("a_qT")
            a_kv = sem("a_kv")
            a_so = sem("a_so")
            a_ro = sem("a_ro")
            a_sk = sem("a_sk")
            a_rms = sem("a_rms")
            a_std = sem("a_std")
            d_x = sem("d_x")
            d_v = sem("d_v")
            d_a = sem("d_a")
            d_q = sem("d_q")
            d_o = sem("d_o")
            d_qp = sem("d_qp")
            d_qT = sem("d_qT")
            d_kv = sem("d_kv")
            d_ro = sem("d_ro")
            d_on = sem("d_on")
            d_k = sem("d_k")
            d_de = sem("d_de")
            d_dr = sem("d_dr")
            d_at = sem("d_at")
            d_st = sem("d_st")
            d_mv = sem("d_mv")
            d_rk = sem("d_rk")
            d_is = sem("d_is")
            d_y = sem("d_y")
            d_kp = sem("d_kp")
            g_qg = sem("g_qg")
            g_qr = sem("g_qr")
            g_h = sem("g_h")
            g_kg = sem("g_kg")
            g_kr = sem("g_kr")

            def steps(eng, step):
                def head(pair, new, old, at_start=False):
                    for p, place in ((0, "first"), (1, "second")):
                        step(2 * pair + p, pair, p, p, place, new, old, at_start)

                def inner(pair0, new, old):
                    with eng.Fori(1, TB // 2) as r:
                        for p in (0, 1):
                            step((2 * pair0 + p) + 2 * r, pair0 + r, p, 2 * r + p, "inner", new, old, False)

                half = TB // 2
                head(0, True, False, True)
                inner(0, True, False)
                head(half, True, True, True)
                inner(half, True, True)
                with eng.Fori(2, TILES // TB) as batch:
                    head(batch * half, True, True)
                    inner(batch * half, True, True)
                head(TILES // 2, False, True)
                inner(TILES // 2, False, True)
                step(TILES + TB, (TILES + TB) // 2, 0, 0, "end", False, False, False)

            def lagging(place, new, old, at_start):
                has_prev = (new and not (at_start and not old and place == "first")) or \
                           (old and not new and place == "first")
                has_done = (old and not (at_start and place == "first")) or place == "end"
                return has_prev, has_done

            block = pa.enter_context(nc.Block())

            @block.sync
            def _(sp):
                for w in range(2):
                    sp.dma_start(w_stage[:, w], w_pieces[w].rearrange("(c p) d -> p c d", p=P)) \
                        .then_inc(weight_in[w], 16)
                for dst, src in ((ident[:, :], identity), (mu[:, 0, :], mu_r.rearrange("(c p) -> p c", p=P)),
                                 (mu[:, 1, :], mu_k.rearrange("(c p) -> p c", p=P)),
                                 (bias_qkv[:, :], b_qkv.partition_broadcast(P)),
                                 (gain_qk[:, :], g_qk.partition_broadcast(P)),
                                 (bias_o[:, :], b_out.partition_broadcast(P)),
                                 (gain_o[:, :], g_out.partition_broadcast(P)),
                                 (cos_t[:, :, :], rope_cos.rearrange("(t p) f -> p t f", p=P)),
                                 (sin_t[:, :, :], rope_sin.rearrange("(t p) f -> p t f", p=P))):
                    sp.dma_start(dst, src, allow_slow_non_contiguous=True).then_inc(const_in, 16)
                for w in range(2, 7):
                    sp.wait_ge(weight_done, w - 1)
                    sp.dma_start(w_stage[:, w % 2], w_pieces[w].rearrange("(c p) d -> p c d", p=P)) \
                        .then_inc(weight_in[w % 2], 16)

                def ahead(count):
                    return count if isinstance(count, int) else sp.snap(count)

                def rows(dram, first):
                    return dram[bass.ds(first if isinstance(first, int) else sp.snap(first), P), :]

                def step(n, pair, p, slot, place, new, old, at_start):
                    has_prev, has_done = lagging(place, new, old, at_start)
                    has_y = has_done and not (at_start and place == "second")
                    x_rows = rows(x, n * P) if new else None
                    ring_slot = slot if isinstance(slot, int) else sp.snap(slot)
                    res_rows = rows(x, n * P - (TB + 1) * P) if has_done else None
                    y_rows = rows(y_mid, n * P - (TB + 2) * P) if has_y else None
                    m1, m7, m9, m10 = (ahead(n - 1), ahead(n - TB + 1), ahead(n - TB - 1), ahead(n - TB - 2))
                    if new:
                        need(sp, t_x, m1)
                        sp.dma_start(x_in[:, p, :], x_rows).then_inc(x_loaded[p], 16)
                    if old:
                        if at_start:
                            sp.wait_ge(g_qr, n - TB + 1)
                        else:
                            sp.wait_ge(t_qT, m9)
                        sp.dma_start(q_tile[:, p, :], q_ring[:, ring_slot, :]).then_inc(q_fetched[p], 16)
                    if has_done:
                        need(sp, g_h, m10)
                        sp.dma_start(x_res[:, 1 - p, :], res_rows) \
                            .then_inc(res_loaded[1 - p], 16)
                    if has_y:
                        sp.wait_ge(d_y, m9)
                        sp.dma_start(y_rows, y_out[:, p, :]) \
                            .then_inc(y_stored[p], 16)

                steps(sp, step)
                sp.wait_ge(d_y, TILES)
                sp.dma_start(y_mid[(TILES - 1) * P:TILES * P, :], y_out[:, (TILES - 1) % 2, :]) \
                    .then_inc(y_stored[(TILES - 1) % 2], 16)
                for p in (0, 1):
                    sp.wait_ge(y_stored[p], 16 * (TILES // 2))

            @block.tensor
            def _(pe):
                def product(psum, lhs_hi, lhs_lo, w):
                    for c in range(KC):
                        nc.tensor.matmul(psum, lhs_hi[:, c, :], wa_hi[:, w, c, :], start=(c == 0), stop=False)
                        nc.tensor.matmul(psum, lhs_hi[:, c, :], wa_lo[:, w, c, :], start=False, stop=False)
                        last = nc.tensor.matmul(psum, lhs_lo[:, c, :], wa_hi[:, w, c, :], start=False,
                                                stop=(c == KC - 1))
                    return last

                def transposed(src):
                    for c in range(KC):
                        last = nc.tensor.transpose(psum_t[:, c * P:(c + 1) * P], src[:, c * P:(c + 1) * P],
                                                   ident[:, :])
                    return last

                pe.wait_ge(const_in, 16 * 9)

                def step(n, pair, p, slot, place, new, old, at_start):
                    has_prev, has_done = lagging(place, new, old, at_start)
                    if new:
                        pe.wait_ge(x_loaded[p], 16 * pair + 16)
                        if old:
                            need(pe, d_qT, n - TB)
                        else:
                            need(pe, d_x, n)
                        transposed(x_in[:, p, :]).then_inc(t_x, 1)
                    if has_prev:
                        need(pe, d_v, n - 1)
                        if at_start and n == 1:
                            pe.wait_ge(weight_done, WV + 1)
                        product(psum_v[:, :], xT_hi[:, 1 - p], xT_lo[:, 1 - p], WV).then_inc(t_v, 1)
                    if has_done:
                        pe.wait_ge(d_at, n - TB)
                        if new:
                            pe.wait_ge(d_x, n + 1)
                        else:
                            pe.wait_ge(d_qT, n - TB)
                        transposed(attn[:, :]).then_inc(t_a, 1)
                    if new:
                        pe.wait_ge(d_x, n + 1)
                        need(pe, d_q, n)
                        if at_start and n == 0:
                            pe.wait_ge(weight_done, WQ + 1)
                        product(psum_q[:, :], xT_hi[:, p], xT_lo[:, p], WQ).then_inc(t_q, 1)
                    if has_done:
                        pe.wait_ge(d_a, n - TB)
                        need(pe, d_o, n - TB - 1)
                        product(psum_o[:, :], aT_hi, aT_lo, WO).then_inc(t_o, 1)
                    if old:
                        pe.wait_ge(q_fetched[p], 16 * pair - 16 * (TB // 2) + 16)
                        if has_done:
                            pe.wait_ge(d_a, n - TB)
                        else:
                            pe.wait_ge(d_x, n + 1)
                        transposed(q_tile[:, p, :]).then_inc(t_qT, 1)
                    if has_prev:
                        pe.wait_ge(a_kf, n)
                        pe.wait_ge(a_v, n)
                        if place == "second":
                            need(pe, d_kv, n - 1)
                        for c in range(NC):
                            for g in range(HC):
                                h = c * HC + g
                                last = nc.tensor.matmul(
                                    kv_cols[g * DH:(g + 1) * DH, c, :], k_feat[:, h * DH:(h + 1) * DH],
                                    v_ext[:, h, :], start=(place == "second" and c == 0),
                                    stop=(place == "first"), skip_group_check=True,
                                    tile_position=(0, g * DH))
                        last.then_inc(t_kv, 1)
                    if new:
                        need(pe, d_k, n)
                        if at_start and n == 0:
                            pe.wait_ge(weight_done, WK + 1)
                        product(psum_k[:, :], xT_hi[:, p], xT_lo[:, p], WK).then_inc(t_k, 1)
                    if old:
                        pe.wait_ge(d_qT, n - TB + 1)
                        if place == "first":
                            pe.wait_ge(d_kv, n)
                        need(pe, d_at, n - TB)
                        for c in range(NC):
                            dst = psum_n[:, c // 2, (c % 2) * HC * EW:(c % 2 + 1) * HC * EW]
                            khi = kv_hi[:, c].rearrange("p g e -> p (g e)")
                            klo = kv_lo[:, c].rearrange("p g e -> p (g e)")
                            nc.tensor.matmul(dst, qT_hi[:, c, :], khi, start=True, stop=False)
                            nc.tensor.matmul(dst, qT_hi[:, c, :], klo, start=False, stop=False)
                            last = nc.tensor.matmul(dst, qT_lo[:, c, :], khi, start=False, stop=True)
                        last.then_inc(t_n, 1)

                steps(pe, step)

            @block.scalar
            def _(act):
                for w in range(7):
                    act.wait_ge(weight_in[w % 2], 16 * (w // 2) + 16)
                    nc.scalar.activation(split[w][0], w_stage[:, w % 2], ACT.Copy).then_inc(weight_hi, 1)
                act.wait_ge(consts_set, 1)

                def step(n, pair, p, slot, place, new, old, at_start):
                    has_prev, has_done = lagging(place, new, old, at_start)
                    if new:
                        act.wait_ge(t_x, n + 1)
                        need(act, t_v, n - 1)
                        nc.scalar.activation(xT_hi[:, p], psum_t[:, :].rearrange("p (c t) -> p c t", c=KC),
                                             ACT.Copy).then_inc(a_x, 1)
                    if has_prev:
                        act.wait_ge(g_kr, n)
                        need(act, t_kv, n - 1)
                        nc.scalar.activation(k_feat[:, :], k_rot[:, :], ACT.Relu).then_inc(a_kf, 1)
                        act.wait_ge(d_rk, n)
                        nc.scalar.activation(v_ext[:, :, DH], ones[:, :], ACT.Copy, scale=inv_rms_k[:, :])
                        act.wait_ge(d_v, n)
                        nc.scalar.activation(v_ext[:, :, 0:DH], v_raw[:, :].rearrange("p (h d) -> p h d", d=DH),
                                             ACT.Copy, scale=inv_rms_k[:, :]).then_inc(a_v, 1)
                    if has_done:
                        act.wait_ge(t_a, n - TB)
                        need(act, t_o, n - TB - 1)
                        nc.scalar.activation(aT_hi[:, :, :], psum_t[:, :].rearrange("p (c t) -> p c t", c=KC),
                                             ACT.Copy).then_inc(a_a, 1)
                    if new:
                        act.wait_ge(d_q, n + 1)
                        need(act, a_rms, n)
                        nc.scalar.activation(squares[:, :], q_raw[:, :], ACT.Square,
                                             accum_out=sum_sq[:, 0:1]).then_inc(a_sq, 1)
                    if has_done:
                        act.wait_ge(d_o, n - TB)
                        if new:
                            act.wait_ge(a_sq, n + 1)
                        nc.scalar.activation(squares[:, :], o_raw[:, :], ACT.Square,
                                             accum_out=sum_sq[:, 2:3]).then_inc(a_so, 1)
                        act.wait_ge(a_so, n - TB)
                        nc.scalar.activation(sum_sq[:, 3:4], sum_sq[:, 2:3], ACT.Sqrt, bias=rms_eps[:, :],
                                             scale=1.0 / D).then_inc(a_ro, 1)
                    if old:
                        act.wait_ge(t_qT, n - TB + 1)
                        need(act, t_n, n - TB)
                        nc.scalar.activation(qT_hi[:, :, :], psum_t[:, :].rearrange("p (c t) -> p c t", c=NC),
                                             ACT.Relu).then_inc(a_qT, 1)
                        if place == "first":
                            act.wait_ge(t_kv, n)
                            for g in range(HC):
                                last = nc.scalar.activation(
                                    kv_hi[g * DH:(g + 1) * DH, :, g, :], kv_cols[g * DH:(g + 1) * DH, :, :],
                                    ACT.Copy)
                            last.then_inc(a_kv, TB)
                    if new:
                        act.wait_ge(d_k, n + 1)
                        act.wait_ge(a_sq, n + 1)
                        if has_done:
                            act.wait_ge(a_so, n - TB)
                        nc.scalar.activation(squares[:, :], k_raw[:, :], ACT.Square,
                                             accum_out=sum_sq[:, 1:2]).then_inc(a_sk, 1)
                        act.wait_ge(a_sk, n + 1)
                        need(act, d_rk, n)
                        nc.scalar.activation(rms_qk[:, :], sum_sq[:, 0:2], ACT.Sqrt, bias=rms_eps[:, :],
                                             scale=1.0 / D).then_inc(a_rms, 1)
                    if has_done:
                        act.wait_ge(d_mv, n - TB)
                        need(act, d_is, n - TB - 1)
                        nc.scalar.activation(std_h[:, :], mean_var[:, 1:2], ACT.Sqrt, bias=ln_eps[:, :]) \
                            .then_inc(a_std, 1)

                steps(act, step)

            @block.vector
            def _(dve):
                for w in range(7):
                    dve.wait_ge(weight_hi, w + 1)
                    nc.vector.tensor_tensor(split[w][1], w_stage[:, w % 2], f32(split[w][0]), ALU.subtract) \
                        .then_inc(weight_done, 1)
                dve.wait_ge(const_in, 16 * 9)
                dve.wait_ge(consts_set, 1)

                def rotate(dst_cos, dst_sin, src, slot):
                    nc.vector.tensor_tensor(
                        dst_cos[:, :].rearrange("p (g f) -> p g f", f=HF), src[:, :].rearrange("p (g f) -> p g f", f=HF),
                        cos_t[:, slot, :].unsqueeze(1).to_broadcast([P, D // HF, HF]), ALU.mult)
                    return nc.vector.tensor_tensor(
                        dst_sin[:, :].rearrange("p (g f) -> p g f", f=DH), src[:, :].rearrange("p (g f) -> p g f", f=DH),
                        sin_t[:, slot, :].unsqueeze(1).to_broadcast([P, D // DH, DH]), ALU.mult)

                def step(n, pair, p, slot, place, new, old, at_start):
                    has_prev, has_done = lagging(place, new, old, at_start)
                    if new:
                        dve.wait_ge(a_x, n + 1)
                        nc.vector.tensor_tensor(xT_lo[:, p], psum_t[:, :].rearrange("p (c t) -> p c t", c=KC),
                                                f32(xT_hi[:, p]), ALU.subtract).then_inc(d_x, 1)
                    if has_prev:
                        dve.wait_ge(t_v, n)
                        need(dve, a_v, n - 1)
                        nc.vector.tensor_tensor(v_raw[:, :], psum_v[:, :], bias_qkv[:, 2 * D:3 * D], ALU.add) \
                            .then_inc(d_v, 1)
                    if has_done:
                        dve.wait_ge(a_a, n - TB)
                        nc.vector.tensor_tensor(aT_lo[:, :, :], psum_t[:, :].rearrange("p (c t) -> p c t", c=KC),
                                                f32(aT_hi[:, :, :]), ALU.subtract).then_inc(d_a, 1)
                    if new:
                        dve.wait_ge(t_q, n + 1)
                        need(dve, a_sq, n)
                        need(dve, g_qg, n)
                        nc.vector.tensor_tensor(q_raw[:, :], psum_q[:, :], bias_qkv[:, 0:D], ALU.add) \
                            .then_inc(d_q, 1)
                        dve.wait_ge(g_qg, n + 1)
                        need(dve, g_qr, n)
                        rotate(q_cos, q_sin, q_g, slot).then_inc(d_qp, 1)
                    if has_done:
                        dve.wait_ge(t_o, n - TB)
                        need(dve, a_so, n - TB - 1)
                        nc.vector.tensor_tensor(o_raw[:, :], psum_o[:, :], bias_o[:, :], ALU.add).then_inc(d_o, 1)
                    if old:
                        dve.wait_ge(a_qT, n - TB + 1)
                        nc.vector.scalar_tensor_tensor(
                            out=qT_lo[:, :, :], in0=psum_t[:, :].rearrange("p (c t) -> p c t", c=NC), scalar=0.0,
                            in1=f32(qT_hi[:, :, :]), op0=ALU.max, op1=ALU.subtract).then_inc(d_qT, 1)
                    if has_done:
                        dve.wait_ge(a_ro, n - TB)
                        nc.vector.reciprocal(inv_rms_o[:, :], sum_sq[:, 3:4]).then_inc(d_ro, 1)
                        dve.wait_ge(d_ro, n - TB)
                        need(dve, g_h, n - TB - 1)
                        nc.vector.scalar_tensor_tensor(out=o_norm[:, :], in0=o_raw[:, :], scalar=inv_rms_o[:, :],
                                                       in1=gain_o[:, :], op0=ALU.mult, op1=ALU.mult) \
                            .then_inc(d_on, 1)
                    if old and place == "first":
                        dve.wait_ge(a_kv, n)
                        for g in range(HC):
                            last = nc.vector.tensor_tensor(
                                kv_lo[g * DH:(g + 1) * DH, :, g, :], kv_cols[g * DH:(g + 1) * DH, :, :],
                                f32(kv_hi[g * DH:(g + 1) * DH, :, g, :]), ALU.subtract)
                        last.then_inc(d_kv, TB)
                    if new:
                        dve.wait_ge(t_k, n + 1)
                        need(dve, a_sk, n)
                        need(dve, g_kg, n)
                        nc.vector.tensor_tensor(k_raw[:, :], psum_k[:, :], bias_qkv[:, D:2 * D], ALU.add) \
                            .then_inc(d_k, 1)
                    if has_done:
                        dve.wait_ge(g_h, n - TB)
                        nc.vector.bn_stats(stats[:, :], h_sum[:, :]).then_inc(d_st, 1)
                        dve.wait_ge(consts_set, 1)
                        dve.wait_ge(d_st, n - TB)
                        nc.vector.bn_aggr(mean_var[:, :], stats[:, :]).then_inc(d_mv, 1)
                    if old:
                        dve.wait_ge(t_n, n - TB + 1)
                        nums = psum_n[:, :, 0:2 * HC * EW].rearrange("p b (h e) -> p b h e", e=EW)
                        den_v = den[:, :, :].rearrange("p s (b h) -> p s b h", b=2)
                        nc.vector.tensor_scalar(den_v[:, 0], nums[:, :, :, DH], eps_q[:, bass.ds(slot, 1)], None,
                                                ALU.add).then_inc(d_de, 1)
                        dve.wait_ge(d_de, n - TB + 1)
                        nc.vector.reciprocal(den[:, 1, :], den[:, 0, :]).then_inc(d_dr, 1)
                        dve.wait_ge(d_dr, n - TB + 1)
                        if has_done:
                            dve.wait_ge(t_a, n - TB)
                        for b in (0, 1):
                            last = nc.vector.tensor_tensor(
                                attn[:, b * D // 2:(b + 1) * D // 2].rearrange("p (h d) -> p h d", d=DH),
                                nums[:, b, :, 0:DH], den_v[:, 1, b].unsqueeze(2).to_broadcast([P, HEADS // 2, DH]),
                                ALU.mult)
                        last.then_inc(d_at, 1)
                    if new:
                        dve.wait_ge(a_rms, n + 1)
                        need(dve, a_v, n)
                        nc.vector.tensor_scalar(eps_q[:, bass.ds(slot, 1)], rms_qk[:, 0:1], EPS_LIN, None, ALU.mult)
                        nc.vector.reciprocal(inv_rms_k[:, :], rms_qk[:, 1:2]).then_inc(d_rk, 1)
                        dve.wait_ge(g_kg, n + 1)
                        need(dve, g_kr, n)
                        rotate(k_cos, k_sin, k_g, slot).then_inc(d_kp, 1)
                    if has_done:
                        dve.wait_ge(a_std, n - TB)
                        nc.vector.reciprocal(inv_std[:, :], std_h[:, :]).then_inc(d_is, 1)
                        dve.wait_ge(d_is, n - TB)
                        if not at_start:
                            dve.wait_ge(y_stored[1 - p], 16 * pair - 16 * (TB // 2 + 1 - p))
                        nc.vector.tensor_scalar(y_out[:, 1 - p, :], h_sum[:, :], mean_var[:, 0:1], inv_std[:, :],
                                                ALU.subtract, ALU.mult).then_inc(d_y, 1)

                steps(dve, step)

            @block.gpsimd
            def _(pool):
                pool.memset(rms_eps[:, :], RMS_EPS)
                pool.memset(ln_eps[:, :], LN_EPS)
                pool.memset(ones[:, :], 1.0)
                pool.memset(kv_hi[:, :, :, :].bitcast(F32), 0.0)
                pool.memset(kv_lo[:, :, :, :].bitcast(F32), 0.0).then_inc(consts_set, 1)
                pool.wait_ge(const_in, 16 * 9)
                pool.wait_ge(weight_done, 7)

                def add_parts(dst, cos_part, sin_part):
                    halves = [t.rearrange("p (h s f) -> p h s f", s=2, f=HF) for t in (dst, cos_part, sin_part)]
                    for s in (0, 1):
                        last = nc.gpsimd.tensor_tensor(halves[0][:, :, s], halves[1][:, :, s],
                                                       halves[2][:, :, 1 - s], ALU.add)
                    return last

                def step(n, pair, p, slot, place, new, old, at_start):
                    has_prev, has_done = lagging(place, new, old, at_start)
                    if new:
                        pool.wait_ge(d_q, n + 1)
                        need(pool, d_qp, n)
                        nc.gpsimd.tensor_tensor(q_g[:, :], q_raw[:, :], gain_qk[:, 0:D], ALU.mult).then_inc(g_qg, 1)
                        pool.wait_ge(d_qp, n + 1)
                        if old:
                            pool.wait_ge(q_fetched[p], 16 * pair - 16 * (TB // 2) + 16)
                        add_parts(q_ring[:, slot, :], q_cos[:, :], q_sin[:, :]).then_inc(g_qr, 1)
                    if has_done:
                        pool.wait_ge(d_on, n - TB)
                        pool.wait_ge(res_loaded[1 - p], 16 * pair - 16 * (TB // 2 - p))
                        need(pool, d_y, n - TB - 1)
                        nc.gpsimd.tensor_tensor(h_sum[:, :], o_norm[:, :], x_res[:, 1 - p, :], ALU.add) \
                            .then_inc(g_h, 1)
                    if new:
                        pool.wait_ge(d_k, n + 1)
                        need(pool, d_kp, n)
                        nc.gpsimd.tensor_tensor(k_g[:, :], k_raw[:, :], gain_qk[:, D:2 * D], ALU.mult).then_inc(g_kg, 1)
                        pool.wait_ge(d_kp, n + 1)
                        need(pool, a_kf, n)
                        add_parts(k_rot[:, :], k_cos[:, :], k_sin[:, :]).then_inc(g_kr, 1)

                steps(pool, step)

        with ExitStack() as pb:
            psum_y = pb.enter_context(nc.psum_tensor("psum_y", [P, 2, BLK], F32))
            psum_u = pb.enter_context(nc.psum_tensor("psum_u", [P, 2, BLK], F32))
            psum_r = pb.enter_context(nc.psum_tensor("psum_r", [P, 2, D], F32))
            psum_w = pb.enter_context(nc.psum_tensor("psum_w", [P, 2, D], F32))
            y_in = sb(pb, "y_in", [P, 2, BT, D])
            yT = sb(pb, "yT", [P, 2, KC, BLK + 1])
            diff = sb(pb, "diff", [P, KC, BLK])
            mix = sb(pb, "mix", [P, 2, BLK])
            xk_hi = sb(pb, "xk_hi", [P, KC, BLK], F32R)
            xk_lo = sb(pb, "xk_lo", [P, KC, BLK], F32R)
            xr_hi = sb(pb, "xr_hi", [P, KC, BLK], F32R)
            xr_lo = sb(pb, "xr_lo", [P, KC, BLK], F32R)
            relu_u = sb(pb, "relu_u", [P, 2, BLK])
            act_u = sb(pb, "act_u", [P, 2, BLK])
            uT_hi = sb(pb, "uT_hi", [P, KC, BLK], F32R)
            uT_lo = sb(pb, "uT_lo", [P, KC, BLK], F32R)
            gate = sb(pb, "gate", [P, BT, D])
            z = sb(pb, "z", [P, BT, D])
            z_stats = sb(pb, "z_stats", [P, BT, 6])
            z_mv = sb(pb, "z_mv", [P, BT, 2])
            z_std = sb(pb, "z_std", [P, BT])
            z_inv = sb(pb, "z_inv", [P, BT])
            z_out = sb(pb, "z_out", [P, BT, D])

            y_loaded = [sem("y_loaded0"), sem("y_loaded1")]
            out_stored = sem("out_stored")
            zero_set = sem("zero_set")
            t_y = sem("t_y")
            t_u = sem("t_u")
            t_r = sem("t_r")
            t_w = sem("t_w")
            a_y = sem("a_y")
            a_c = sem("a_c")
            a_mh = sem("a_mh")
            a_ru = sem("a_ru")
            a_uh = sem("a_uh")
            a_zs = sem("a_zs")
            a_g = sem("a_g")
            d_m = sem("d_m")
            d_ml = sem("d_ml")
            d_z = sem("d_z")
            d_zs = sem("d_zs")
            d_zm = sem("d_zm")
            d_ul = sem("d_ul")
            d_zi = sem("d_zi")
            d_zo = sem("d_zo")
            g_d = sem("g_d")
            g_z = sem("g_z")
            g_u = sem("g_u")

            def blocks(eng, step):
                for s in (0, 1):
                    step(s, 0, s, s == 0)
                with eng.Fori(1, BLOCKS // BPB) as b:
                    for s in (0, 1):
                        step(2 * b + s, b, s, False)
                step(BLOCKS, BLOCKS // BPB, 0, False)

            block = pb.enter_context(nc.Block())

            @block.sync
            def _(sp):
                def tokens(dram, m):
                    first = m * BLK if isinstance(m, int) else sp.snap(m * BLK)
                    return dram[bass.ds(first, BLK), :].rearrange("(t p) d -> p t d", p=P)

                def step(m, b, s, first):
                    more = not (isinstance(m, int) and m == BLOCKS)
                    done = not (isinstance(m, int) and m < 2)
                    y_rows = tokens(y_mid, m) if more else None
                    out_rows = tokens(out, m - 2) if done else None
                    used, before = (v if isinstance(v, int) else sp.snap(v) for v in (BT * m - BT, m - 1))
                    if more:
                        need(sp, g_z, used)
                        sp.dma_start(y_in[:, s], y_rows).then_inc(y_loaded[s], 16)
                    if done:
                        sp.wait_ge(d_zo, before)
                        sp.dma_start(out_rows, z_out[:, :, :]).then_inc(out_stored, 16)

                blocks(sp, step)
                sp.wait_ge(d_zo, BLOCKS)
                sp.dma_start(tokens(out, BLOCKS - 1), z_out[:, :, :]).then_inc(out_stored, 16)
                sp.wait_ge(out_stored, 16 * BLOCKS)

            @block.tensor
            def _(pe):
                def product(psum, lhs_hi, lhs_lo, rhs_hi, rhs_lo):
                    for c in range(KC):
                        nc.tensor.matmul(psum, lhs_hi(c), rhs_hi(c), start=(c == 0), stop=False)
                        nc.tensor.matmul(psum, lhs_hi(c), rhs_lo(c), start=False, stop=False)
                        last = nc.tensor.matmul(psum, lhs_lo(c), rhs_hi(c), start=False, stop=(c == KC - 1))
                    return last

                def step(m, b, s, first):
                    more = not (isinstance(m, int) and m == BLOCKS)
                    if more:
                        pe.wait_ge(y_loaded[s], 16 * b + 16)
                        for c in range(KC):
                            need(pe, a_y, KC * m + c - 1)
                            for t in range(BT):
                                last = nc.tensor.transpose(psum_y[:, c % 2, t * P:(t + 1) * P],
                                                           y_in[:, s, t, c * P:(c + 1) * P], ident[:, :])
                            last.then_inc(t_y, 1)
                    if not first:
                        pe.wait_ge(d_ul, KC * m)
                        for t in range(BT):
                            need(pe, d_z, BT * m - BT + t - 1)
                            tok = slice(t * P, (t + 1) * P)
                            product(psum_w[:, t % 2, :], lambda c: uT_hi[:, c, tok], lambda c: uT_lo[:, c, tok],
                                    lambda c: wb_hi[:, WVF, c, :], lambda c: wb_lo[:, WVF, c, :]).then_inc(t_w, 1)
                    if more:
                        pe.wait_ge(d_ml, 2 * KC * m + KC)
                        for o in range(KC):
                            need(pe, a_ru, KC * m + o - 1)
                            feat = slice(o * P, (o + 1) * P)
                            product(psum_u[:, o % 2, :], lambda c: wb_hi[:, WKF, c, feat],
                                    lambda c: wb_lo[:, WKF, c, feat], lambda c: xk_hi[:, c, :],
                                    lambda c: xk_lo[:, c, :]).then_inc(t_u, 1)
                        pe.wait_ge(d_ml, 2 * KC * m + 2 * KC)
                        for t in range(BT):
                            need(pe, a_g, BT * m + t - 1)
                            tok = slice(t * P, (t + 1) * P)
                            product(psum_r[:, t % 2, :], lambda c: xr_hi[:, c, tok], lambda c: xr_lo[:, c, tok],
                                    lambda c: wb_hi[:, WR, c, :], lambda c: wb_lo[:, WR, c, :]).then_inc(t_r, 1)

                blocks(pe, step)

            @block.scalar
            def _(act):
                def step(m, b, s, first):
                    more = not (isinstance(m, int) and m == BLOCKS)
                    if more:
                        need(act, d_m, 2 * KC * m - 2 * KC)
                        if s == 1:
                            act.wait_ge(a_y, KC * m)
                            nc.scalar.activation(yT[:, 1, :, 0], yT[:, 0, :, BLK], ACT.Copy).then_inc(a_c, 1)
                        for c in range(KC):
                            act.wait_ge(t_y, KC * m + c + 1)
                            nc.scalar.activation(yT[:, s, c, 1:BLK + 1], psum_y[:, c % 2, :], ACT.Copy) \
                                .then_inc(a_y, 1)
                        for i in range(2 * KC):
                            c, hi = i % KC, (xk_hi, xr_hi)[i // KC]
                            if i == 0:
                                need(act, t_u, KC * m)
                            if i == KC:
                                need(act, t_r, BT * m)
                            act.wait_ge(d_m, 2 * KC * m + i + 1)
                            nc.scalar.activation(hi[:, c, :], mix[:, i % 2, :], ACT.Copy).then_inc(a_mh, 1)
                        need(act, t_w, BT * m)
                        for o in range(KC):
                            act.wait_ge(t_u, KC * m + o + 1)
                            need(act, g_u, KC * m + o - 1)
                            nc.scalar.activation(relu_u[:, o % 2, :], psum_u[:, o % 2, :], ACT.Relu) \
                                .then_inc(a_ru, 1)
                            act.wait_ge(a_ru, KC * m + o + 1)
                            nc.scalar.activation(uT_hi[:, o, :], relu_u[:, o % 2, :], ACT.Square).then_inc(a_uh, 1)
                    if not first:
                        act.wait_ge(d_zm, BT * m)
                        nc.scalar.activation(z_std[:, :], z_mv[:, :, 1], ACT.Sqrt, bias=ln_eps[:, :]) \
                            .then_inc(a_zs, 1)
                    if more:
                        need(act, d_z, BT * m)
                        for t in range(BT):
                            act.wait_ge(t_r, BT * m + t + 1)
                            nc.scalar.activation(gate[:, t, :], psum_r[:, t % 2, :], ACT.Sigmoid).then_inc(a_g, 1)

                blocks(act, step)

            @block.vector
            def _(dve):
                dve.wait_ge(zero_set, 1)

                def step(m, b, s, first):
                    more = not (isinstance(m, int) and m == BLOCKS)

                    def low(i):
                        c, hi, lo = i % KC, (xk_hi, xr_hi)[i // KC], (xk_lo, xr_lo)[i // KC]
                        dve.wait_ge(a_mh, 2 * KC * m + i + 1)
                        nc.vector.tensor_tensor(lo[:, c, :], mix[:, i % 2, :], f32(hi[:, c, :]), ALU.subtract) \
                            .then_inc(d_ml, 1)

                    for i in range(2 * KC):
                        c = i % KC
                        if more:
                            if i < KC:
                                dve.wait_ge(g_d, KC * m + c + 1)
                            if i >= 2:
                                dve.wait_ge(d_ml, 2 * KC * m + i - 1)
                            nc.vector.scalar_tensor_tensor(
                                out=mix[:, i % 2, :], in0=diff[:, c, :], scalar=mu[:, 1 - i // KC, c:c + 1],
                                in1=yT[:, s, c, 0:BLK], op0=ALU.mult, op1=ALU.add).then_inc(d_m, 1)
                            if i:
                                low(i - 1)
                        if not first and i % 2:
                            t = i // 2
                            dve.wait_ge(t_w, BT * m - BT + t + 1)
                            if t == 0:
                                dve.wait_ge(a_g, BT * m)
                                need(dve, d_zo, m - 1)
                            nc.vector.tensor_tensor(z[:, t, :], psum_w[:, t % 2, :], gate[:, t, :], ALU.mult) \
                                .then_inc(d_z, 1)
                    if more:
                        low(2 * KC - 1)
                    if not first:
                        for t in range(BT):
                            dve.wait_ge(g_z, BT * m - BT + t + 1)
                            nc.vector.bn_stats(z_stats[:, t, :], z[:, t, :]).then_inc(d_zs, 1)
                        for t in range(BT):
                            dve.wait_ge(zero_set, 1)
                            dve.wait_ge(d_zs, BT * m - BT + t + 1)
                            nc.vector.bn_aggr(z_mv[:, t, :], z_stats[:, t, :]).then_inc(d_zm, 1)
                    if more:
                        for o in range(KC):
                            dve.wait_ge(a_uh, KC * m + o + 1)
                            dve.wait_ge(g_u, KC * m + o + 1)
                            nc.vector.tensor_tensor(uT_lo[:, o, :], act_u[:, o % 2, :], f32(uT_hi[:, o, :]),
                                                    ALU.subtract).then_inc(d_ul, 1)
                    if not first:
                        dve.wait_ge(a_zs, m)
                        nc.vector.reciprocal(z_inv[:, :], z_std[:, :]).then_inc(d_zi, 1)
                        dve.wait_ge(d_zi, m)
                        if not (isinstance(m, int) and m == 1):
                            dve.wait_ge(out_stored, 16 * m - 16)
                        for t in range(BT):
                            last = nc.vector.tensor_scalar(z_out[:, t, :], z[:, t, :], z_mv[:, t, 0:1],
                                                           z_inv[:, t:t + 1], ALU.subtract, ALU.mult)
                        last.then_inc(d_zo, 1)

                blocks(dve, step)

            @block.gpsimd
            def _(pool):
                pool.memset(yT[:, 0, :, 0:1], 0.0).then_inc(zero_set, 1)
                pool.wait_ge(zero_set, 1)

                def step(m, b, s, first):
                    more = not (isinstance(m, int) and m == BLOCKS)
                    if more:
                        need(pool, d_m, 2 * KC * m)
                        if s == 1:
                            pool.wait_ge(a_c, b + 1)
                        for c in range(KC):
                            pool.wait_ge(a_y, KC * m + c + 1)
                            nc.gpsimd.tensor_tensor(diff[:, c, :], yT[:, s, c, 1:BLK + 1], yT[:, s, c, 0:BLK],
                                                    ALU.subtract).then_inc(g_d, 1)
                    if not first:
                        for t in range(BT):
                            pool.wait_ge(d_z, BT * m - BT + t + 1)
                            nc.gpsimd.tensor_tensor(z[:, t, :], z[:, t, :], y_in[:, 1 - s, t, :], ALU.add) \
                                .then_inc(g_z, 1)
                    if more:
                        for o in range(KC):
                            pool.wait_ge(a_ru, KC * m + o + 1)
                            need(pool, d_ul, KC * m + o - 1)
                            nc.gpsimd.tensor_tensor(act_u[:, o % 2, :], relu_u[:, o % 2, :], relu_u[:, o % 2, :],
                                                    ALU.mult).then_inc(g_u, 1)

                blocks(pool, step)


_FROM_REFERENCE = {"x": "L0_attn_x", "w_r": "L0_ffn_W_r", "w_k": "L0_ffn_W_k", "w_v": "L0_ffn_W_v",
                   "mu_r": "L0_ffn_mu_r", "mu_k": "L0_ffn_mu_k"}


def kernel(**inputs):
    import concourse.bacc as bacc
    from concourse.bass_utils import run_bass_kernel_spmd

    given = {name: np.asarray(a) for name, a in inputs.items()}
    x = given["L0_attn_x"]
    B, L, D = x.shape
    DH = D // HEADS
    order = np.arange(D).reshape(HEADS, DH // 2, 2).transpose(0, 2, 1).reshape(D)
    order_qkv = np.concatenate([order, D + order, 2 * D + np.arange(D)])
    inv_freq = (1.0 / np.float32(10000.0) ** (np.arange(0, DH, 2, dtype=np.float32) / np.float32(DH))).astype(np.float32)
    angles = np.outer(np.arange(L, dtype=np.float32), inv_freq).astype(np.float32)
    cos, sin = np.cos(angles), np.sin(angles)

    def laid(a):
        return np.ascontiguousarray(a)

    arrays = {
        "x": laid(x.reshape(B * L, D)),
        "w_qkv": laid(given["L0_attn_Wqkv"][order_qkv].T),
        "b_qkv": laid(given["L0_attn_bqkv"][order_qkv]),
        "g_qk": laid(np.concatenate([given["L0_attn_gq"][order], given["L0_attn_gk"][order]])),
        "w_out": laid(given["L0_attn_Wout"].T),
        "b_out": laid(given["L0_attn_bout"]),
        "g_out": laid(given["L0_attn_gout"]),
        "w_r": laid(given["L0_ffn_W_r"].T),
        "w_k": laid(given["L0_ffn_W_k"].T),
        "w_v": laid(given["L0_ffn_W_v"].T),
        "mu_r": laid(given["L0_ffn_mu_r"]),
        "mu_k": laid(given["L0_ffn_mu_k"]),
        "rope_cos": laid(cos),
        "rope_sin": laid(np.concatenate([sin, -sin], axis=1)),
        "identity": np.eye(P, dtype=np.float32),
    }
    nc = bacc.Bacc("TRN2", target_bir_lowering=False, num_devices=1, dynamic_dma_scratch_size=1024)
    args = {n: nc.dram_tensor(n, a.shape, mybir.dt.from_np(a.dtype), kind="ExternalInput").ap() for n, a in arrays.items()}
    out = nc.dram_tensor("out", (B * L, D), F32, kind="ExternalOutput").ap()
    y_mid = nc.dram_tensor("y_mid", (B * L, D), F32, kind="Internal").ap()
    postnorm_layer(nc, **args, out=out, y_mid=y_mid)
    r = run_bass_kernel_spmd(nc, [arrays], core_ids=[0])
    return r.results[0]["out"].reshape(B, L, D)
```

```python
from contextlib import ExitStack

import numpy as np

import concourse.bass as bass
from concourse import mybir

ALU = mybir.AluOpType
ACT = mybir.ActivationFunctionType
F32 = mybir.dt.float32
F32R = mybir.dt.float32r

P = 128
HEADS = 16
RMS_EPS = 1.1920929e-07
EPS_LIN = 1e-06
LN_EPS = 1e-05


def need(eng, sem, count):
    if not isinstance(count, int) or count > 0:
        eng.wait_ge(sem, count)


def f32(ap):
    return ap.bitcast(F32)


def postnorm_layer(nc, x, x_T, w_qkv, b_qkv, g_qk, w_out, b_out, g_out, w_r, w_k, w_v, mu_r, mu_k,
                   rope_cos, rope_sin, identity, out, y_mid):
    TOKENS, D = x.shape
    L = rope_cos.shape[0]
    KC = D // P
    DH = D // HEADS
    HF = DH // 2
    HC = P // DH
    NC = HEADS // HC
    EW = DH + 1
    TILES = TOKENS // P
    TB = L // P
    assert TB % 2 == 0 and TILES % TB == 0
    BT = 4
    BLK = BT * P
    BLOCKS = TOKENS // BLK
    BPB = L // BLK
    assert BPB == 2

    ctx = ExitStack()

    def sb(scope, name, shape, dt=F32):
        return scope.enter_context(nc.sbuf_tensor(name, shape, dt))

    def sem(name):
        return ctx.enter_context(nc.semaphore(name))

    with ctx:
        WR, WKF, WVF = range(3)
        wb_hi = sb(ctx, "wb_hi", [P, 3, KC, D], F32R)
        wb_lo = sb(ctx, "wb_lo", [P, 3, KC, D], F32R)
        ln_eps = sb(ctx, "ln_eps", [P, 1])
        y_in = sb(ctx, "y_in", [P, 2, BT, D])
        y_loaded = [sem("y_loaded0"), sem("y_loaded1")]
        y_out = sb(ctx, "y_out", [P, 2, D])
        y_stored = [sem("y_stored0"), sem("y_stored1")]

        def block_rows(dram, m):
            return dram[bass.ds(m * BLK if isinstance(m, int) else m, BLK), :].rearrange("(t p) d -> p t d", p=P)

        ident = sb(ctx, "ident", [P, P])
        mu = sb(ctx, "mu", [P, 2, KC])
        w_pieces = [w_qkv[:, 0:D], w_qkv[:, D:2 * D], w_qkv[:, 2 * D:3 * D], w_out, w_r, w_k, w_v]

        weight_in = [sem(f"weight_in{w}") for w in range(len(w_pieces))]
        ident_in = sem("ident_in")
        const_in = sem("const_in")
        weight_hi = sem("weight_hi")
        weight_done = sem("weight_done")

        with ExitStack() as pa:
            WQ, WK, WV, WO = range(4)
            wa_hi = sb(pa, "wa_hi", [P, 4, KC, D], F32R)
            wa_lo = sb(pa, "wa_lo", [P, 4, KC, D], F32R)
            split = [(wa_hi[:, w], wa_lo[:, w]) for w in range(4)] + [(wb_hi[:, w], wb_lo[:, w]) for w in range(3)]
            rms_eps = sb(pa, "rms_eps", [P, 1])
            psum_q = pa.enter_context(nc.psum_tensor("psum_q", [P, D], F32))
            psum_k = pa.enter_context(nc.psum_tensor("psum_k", [P, D], F32))
            psum_v = pa.enter_context(nc.psum_tensor("psum_v", [P, D], F32))
            psum_o = pa.enter_context(nc.psum_tensor("psum_o", [P, D], F32))
            psum_t = pa.enter_context(nc.psum_tensor("psum_t", [P, D], F32))
            psum_kv = pa.enter_context(nc.psum_tensor("psum_kv", [P, D], F32))
            psum_n = pa.enter_context(nc.psum_tensor("psum_n", [P, 2, D], F32))
            kv_cols = psum_kv[:, 0:NC * EW].rearrange("p (c e) -> p c e", e=EW)

            bias_qkv = sb(pa, "bias_qkv", [P, 3 * D])
            gain_qk = sb(pa, "gain_qk", [P, 2 * D])
            bias_o = sb(pa, "bias_o", [P, D])
            gain_o = sb(pa, "gain_o", [P, D])
            cos_t = sb(pa, "cos_t", [P, TB, HF])
            sin_t = sb(pa, "sin_t", [P, TB, DH])
            ones = sb(pa, "ones", [P, HEADS])
            xT_in = sb(pa, "xT_in", [P, 2, KC, P])
            x_res = sb(pa, "x_res", [P, D])
            xT_hi = sb(pa, "xT_hi", [P, 2, KC, P], F32R)
            xT_lo = sb(pa, "xT_lo", [P, 2, KC, P], F32R)
            q_raw = sb(pa, "q_raw", [P, D])
            k_raw = sb(pa, "k_raw", [P, D])
            v_raw = sb(pa, "v_raw", [P, D])
            q_g = sb(pa, "q_g", [P, D])
            k_g = sb(pa, "k_g", [P, D])
            q_cos = sb(pa, "q_cos", [P, D])
            q_sin = sb(pa, "q_sin", [P, D])
            k_cos = sb(pa, "k_cos", [P, D])
            k_sin = sb(pa, "k_sin", [P, D])
            q_ring = sb(pa, "q_ring", [P, TB, D])
            q_tile = sb(pa, "q_tile", [P, 2, D])
            k_rot = sb(pa, "k_rot", [P, D])
            k_feat = sb(pa, "k_feat", [P, D])
            v_ext = sb(pa, "v_ext", [P, HEADS, EW])
            squares = sb(pa, "squares", [P, D])
            sum_sq = sb(pa, "sum_sq", [P, 4])
            rms_qk = sb(pa, "rms_qk", [P, 2])
            inv_rms_k = sb(pa, "inv_rms_k", [P, 1])
            eps_q = sb(pa, "eps_q", [P, TB])
            qT_feat = sb(pa, "qT_feat", [P, NC, P])
            kv_diag = sb(pa, "kv_diag", [P, NC, HC, EW])
            den = sb(pa, "den", [P, 2, HEADS])
            attn = sb(pa, "attn", [P, D])
            aT_hi = sb(pa, "aT_hi", [P, KC, P], F32R)
            aT_lo = sb(pa, "aT_lo", [P, KC, P], F32R)
            o_raw = sb(pa, "o_raw", [P, D])
            h_sum = sb(pa, "h_sum", [P, D])
            inv_rms_o = sb(pa, "inv_rms_o", [P, 1])
            stats = sb(pa, "stats", [P, 6])
            mean_var = sb(pa, "mean_var", [P, 2])
            std_h = sb(pa, "std_h", [P, 1])
            inv_std = sb(pa, "inv_std", [P, 1])
            w_stage = [q_ring[:, 0:KC, :], q_ring[:, KC:2 * KC, :]] + [y_in[:, 1]] * 5
            CONSTS = 6

            x_loaded = [sem("x_loaded0"), sem("x_loaded1")]
            res_loaded = sem("res_loaded")
            q_fetched = [sem("q_fetched0"), sem("q_fetched1")]
            consts_set = sem("consts_set")
            t_v = sem("t_v")
            t_a = sem("t_a")
            t_q = sem("t_q")
            t_o = sem("t_o")
            t_qT = sem("t_qT")
            t_kv = sem("t_kv")
            t_k = sem("t_k")
            t_n = sem("t_n")
            a_x = sem("a_x")
            a_v = sem("a_v")
            a_kf = sem("a_kf")
            a_a = sem("a_a")
            a_sq = sem("a_sq")
            a_qT = sem("a_qT")
            a_kv = sem("a_kv")
            a_so = sem("a_so")
            a_ro = sem("a_ro")
            a_sk = sem("a_sk")
            a_rms = sem("a_rms")
            a_std = sem("a_std")
            d_x = sem("d_x")
            d_v = sem("d_v")
            d_a = sem("d_a")
            d_q = sem("d_q")
            d_o = sem("d_o")
            d_qp = sem("d_qp")
            d_ro = sem("d_ro")
            d_on = sem("d_on")
            d_k = sem("d_k")
            d_de = sem("d_de")
            d_dr = sem("d_dr")
            d_at = sem("d_at")
            d_st = sem("d_st")
            d_mv = sem("d_mv")
            d_rk = sem("d_rk")
            d_is = sem("d_is")
            d_y = sem("d_y")
            d_kp = sem("d_kp")
            g_qg = sem("g_qg")
            g_qr = sem("g_qr")
            g_h = sem("g_h")
            g_kg = sem("g_kg")
            g_kr = sem("g_kr")

            def steps(eng, step):
                half = TB // 2

                def static(n):
                    t = n % TB
                    step(n, n // 2, n % 2, t, (t - 1) % TB, ("first", "second")[t] if t < 2 else "inner",
                         lambda lag: 0 <= n - lag < TILES)

                def head(batch):
                    for p, place in ((0, "first"), (1, "second")):
                        step(2 * half * batch + p, half * batch, p, p, (p - 1) % TB, place, lambda lag: True)

                def inner(batch, has, pairs=half):
                    with eng.Fori(1, pairs) as r:
                        for p in (0, 1):
                            step((TB * batch + p) + 2 * r, half * batch + r, p, 2 * r + p, 2 * r + (p - 1),
                                 "inner", has)

                static(0)
                static(1)
                inner(0, lambda lag: lag < TB)
                static(TB)
                static(TB + 1)
                inner(1, lambda lag: True)
                with eng.Fori(2, TILES // TB) as batch:
                    head(batch)
                    inner(batch, lambda lag: True)
                static(TILES)
                static(TILES + 1)
                inner(TILES // TB, lambda lag: lag >= TB - 1, half - 1)
                for n in range(TILES + TB - 2, TILES + TB + 2):
                    static(n)

            split_behind = {0: 2, 1: 3, TB: 4, TB + 1: 5, TILES: 6}

            def qT_lags(n, has):
                if isinstance(n, int) and n == TILES:
                    return TB, TB - 1
                lag = TB if has(0) else TB - 1
                return (lag,) if has(lag) else ()

            def parity(p, lag):
                return p if lag % 2 == 0 else 1 - p

            block = pa.enter_context(nc.Block())

            @block.sync
            def _(sp):
                def load_weight(w):
                    sp.dma_start(w_stage[w], w_pieces[w].rearrange("(c p) d -> p c d", p=P)).then_inc(weight_in[w], 16)

                sp.dma_start(ident[:, :], identity).then_inc(ident_in, 16)
                load_weight(0)
                consts = ((mu[:, 0, :], mu_r.rearrange("(c p) -> p c", p=P)),
                          (mu[:, 1, :], mu_k.rearrange("(c p) -> p c", p=P)),
                          (bias_qkv[:, :], b_qkv.partition_broadcast(P)),
                          (gain_qk[:, :], g_qk.partition_broadcast(P)),
                          (cos_t[:, :, :], rope_cos.rearrange("(t p) f -> p t f", p=P)),
                          (sin_t[:, :, :], rope_sin.rearrange("(t p) f -> p t f", p=P)))
                assert len(consts) == CONSTS

                def ahead(count):
                    return count if isinstance(count, int) else sp.snap(count)

                def rows(dram, first):
                    return dram[bass.ds(ahead(first), P), :]

                def step(n, pair, p, slot, before, place, has):
                    tile = x_T[bass.ds(ahead(n), 1)].rearrange("n p c t -> (n p) c t") if has(0) else None
                    ring_slot = ahead(slot)
                    next_slot = (slot + 1) % TB if isinstance(slot, int) else ahead(slot + 1)
                    res_rows = rows(x, n * P - (TB + 1) * P) if has(TB + 1) else None
                    m1, m8, m9 = ahead(n - 1), ahead(n - TB), ahead(n - TB - 1)
                    if has(0):
                        need(sp, d_x, m1)
                        sp.dma_start(xT_in[:, p], tile).then_inc(x_loaded[p], 16)
                    if isinstance(n, int) and split_behind.get(n, 0) > 2:
                        w = split_behind[n]
                        sp.wait_ge(weight_done, w)
                        load_weight(w)
                    if isinstance(n, int) and n == 0:
                        for dst, src in consts:
                            sp.dma_start(dst, src, allow_slow_non_contiguous=True).then_inc(const_in, 16)
                        load_weight(1)
                        load_weight(2)
                        sp.dma_start(bias_o[:, :], b_out.partition_broadcast(P)).then_inc(y_stored[0], 16)
                        sp.dma_start(gain_o[:, :], g_out.partition_broadcast(P)).then_inc(y_stored[1], 16)
                    for lag in qT_lags(n, has):
                        if isinstance(n, int) and n <= TB + 1:
                            sp.wait_ge(g_qr, n - TB + 1)
                        elif has(0):
                            sp.wait_ge(t_qT, m9)
                        else:
                            sp.wait_ge(t_qT, m9 if lag == TB else m8)
                        sp.dma_start(q_tile[:, parity(p, lag), :], q_ring[:, ring_slot if lag == TB else next_slot, :]) \
                            .then_inc(q_fetched[parity(p, lag)], 16)
                    if has(TB + 1):
                        need(sp, g_h, m9)
                        sp.dma_start(x_res[:, :], res_rows).then_inc(res_loaded, 16)
                    if isinstance(n, int) and TILES <= n < TILES + 2:
                        for s in (0, 1):
                            sp.wait_ge(y_stored[s], 16 * (BT * (n - TILES + 1) // 2) + 16)
                        if p == 1:
                            sp.wait_ge(weight_done, len(w_pieces))
                        sp.dma_start(y_in[:, p], block_rows(y_mid, n - TILES)).then_inc(y_loaded[p], 16)

                steps(sp, step)

            @block.tensor
            def _(pe):
                def product(psum, lhs_hi, lhs_lo, w):
                    for c in range(KC):
                        nc.tensor.matmul(psum, lhs_hi[:, c, :], wa_hi[:, w, c, :], start=(c == 0), stop=False)
                        nc.tensor.matmul(psum, lhs_hi[:, c, :], wa_lo[:, w, c, :], start=False, stop=False)
                        last = nc.tensor.matmul(psum, lhs_lo[:, c, :], wa_hi[:, w, c, :], start=False,
                                                stop=(c == KC - 1))
                    return last

                def transposed(psum, src):
                    for c in range(KC):
                        last = nc.tensor.transpose(psum[:, c * P:(c + 1) * P], src[:, c * P:(c + 1) * P],
                                                   ident[:, :])
                    return last

                def weight_ready(n, at, w):
                    if isinstance(n, int) and n == at:
                        pe.wait_ge(weight_done, w + 1)

                pe.wait_ge(ident_in, 16)

                def step(n, pair, p, slot, before, place, has):
                    tail, head_of_tail = not has(0), isinstance(n, int) and n == TILES
                    if has(1):
                        need(pe, d_v, n - 1)
                        weight_ready(n, 1, WV)
                        product(psum_v[:, :], xT_hi[:, 1 - p], xT_lo[:, 1 - p], WV).then_inc(t_v, 1)
                    def attn_T():
                        pe.wait_ge(d_at, n - TB)
                        if not tail or head_of_tail:
                            pe.wait_ge(a_qT, n - TB)
                        else:
                            pe.wait_ge(d_a, n - TB - 1)
                        transposed(psum_t, attn[:, :]).then_inc(t_a, 1)

                    def q_T(lag):
                        pe.wait_ge(q_fetched[parity(p, lag)], 16 * pair - 16 * (TB // 2) + (
                            32 if p == 1 and lag == TB - 1 else 16))
                        if not tail:
                            if has(TB + 1):
                                pe.wait_ge(d_a, n - TB)
                        elif lag == TB:
                            pe.wait_ge(d_q, TILES)
                        else:
                            pe.wait_ge(a_qT, n - TB + 1)
                        transposed(psum_q if tail else psum_t, q_tile[:, parity(p, lag), :]).then_inc(t_qT, 1)

                    def projection():
                        pe.wait_ge(d_a, n - TB)
                        need(pe, d_o, n - TB - 1)
                        weight_ready(n, TB + 1, WO)
                        product(psum_o[:, :], aT_hi, aT_lo, WO).then_inc(t_o, 1)

                    def numerators():
                        pe.wait_ge(a_qT, n - TB + 1)
                        if place == "first":
                            pe.wait_ge(a_kv, n)
                        need(pe, d_at, n - TB)
                        for c in range(NC):
                            last = nc.tensor.matmul(
                                psum_n[:, c // 2, (c % 2) * HC * EW:(c % 2 + 1) * HC * EW], qT_feat[:, c, :],
                                kv_diag[:, c].rearrange("p g e -> p (g e)"), start=True, stop=True)
                        last.then_inc(t_n, 1)

                    if has(TB + 1):
                        attn_T()
                    if tail and not head_of_tail:
                        if has(TB):
                            numerators()
                        if has(TB - 1):
                            q_T(TB - 1)
                        if has(TB + 1):
                            projection()
                        return
                    if head_of_tail:
                        q_T(TB)
                    if has(0):
                        pe.wait_ge(d_x, n + 1)
                        need(pe, d_q, n)
                        weight_ready(n, 0, WQ)
                        product(psum_q[:, :], xT_hi[:, p], xT_lo[:, p], WQ).then_inc(t_q, 1)
                    if has(TB + 1):
                        projection()
                    if has(TB):
                        q_T(TB - 1 if head_of_tail else TB)
                    if has(1):
                        pe.wait_ge(a_kf, n)
                        if place == "second":
                            need(pe, a_kv, n - 1)
                        for c in range(NC):
                            for g in range(HC):
                                h = c * HC + g
                                last = nc.tensor.matmul(
                                    kv_cols[g * DH:(g + 1) * DH, c, :], k_feat[:, h * DH:(h + 1) * DH],
                                    v_ext[:, h, :], start=(place == "second" and c == 0),
                                    stop=(place == "first"), skip_group_check=True,
                                    tile_position=(0, g * DH))
                        last.then_inc(t_kv, 1)
                    if has(0):
                        need(pe, d_k, n)
                        weight_ready(n, 0, WK)
                        product(psum_k[:, :], xT_hi[:, p], xT_lo[:, p], WK).then_inc(t_k, 1)
                    if has(TB):
                        numerators()

                steps(pe, step)

            @block.scalar
            def _(act):
                def weight_high(w):
                    act.wait_ge(weight_in[w], 16)
                    nc.scalar.activation(split[w][0], w_stage[w], ACT.Copy).then_inc(weight_hi, 1)

                def chunks(psum):
                    return psum[:, :].rearrange("p (c t) -> p c t", t=P)

                weight_high(0)

                def step(n, pair, p, slot, before, place, has):
                    tail, head_of_tail = not has(0), isinstance(n, int) and n == TILES

                    def q_feature(lag):
                        act.wait_ge(t_qT, n - lag + 1)
                        need(act, t_n, n - lag)
                        nc.scalar.activation(qT_feat[:, :, :], chunks(psum_q if tail else psum_t), ACT.Relu) \
                            .then_inc(a_qT, 1)

                    if has(TB + 2):
                        row = n * P - (TB + 2) * P
                        y_rows = y_mid[bass.ds(row if isinstance(row, int) else act.snap(row), P), :]
                    if has(0):
                        act.wait_ge(x_loaded[p], 16 * pair + 16)
                        need(act, t_v, n - 1)
                        nc.scalar.activation(xT_hi[:, p], xT_in[:, p], ACT.Copy).then_inc(a_x, 1)
                    if isinstance(n, int) and n == 0:
                        weight_high(1)
                        act.wait_ge(consts_set, 1)
                    if has(TB + 1):
                        act.wait_ge(t_a, n - TB)
                        need(act, t_o, n - TB - 1)
                        nc.scalar.activation(aT_hi[:, :, :], chunks(psum_t), ACT.Copy).then_inc(a_a, 1)
                    if tail and not head_of_tail and has(TB - 1):
                        q_feature(TB - 1)
                    if has(1):
                        act.wait_ge(d_rk, n)
                        need(act, t_kv, n - 1)
                        nc.scalar.activation(v_ext[:, :, DH], ones[:, :], ACT.Copy, scale=inv_rms_k[:, :])
                        act.wait_ge(d_v, n)
                        nc.scalar.activation(v_ext[:, :, 0:DH], v_raw[:, :].rearrange("p (h d) -> p h d", d=DH),
                                             ACT.Copy, scale=inv_rms_k[:, :]).then_inc(a_v, 1)
                        act.wait_ge(g_kr, n)
                        nc.scalar.activation(k_feat[:, :], k_rot[:, :], ACT.Relu).then_inc(a_kf, 1)
                    if has(TB + 2):
                        act.wait_ge(d_mv, n - TB - 1)
                        need(act, d_is, n - TB - 2)
                        nc.scalar.activation(std_h[:, :], mean_var[:, 1:2], ACT.Sqrt, bias=ln_eps[:, :]) \
                            .then_inc(a_std, 1)
                    if has(0):
                        act.wait_ge(d_q, n + 1)
                        need(act, a_rms, n)
                        nc.scalar.activation(squares[:, :], q_raw[:, :], ACT.Square,
                                             accum_out=sum_sq[:, 0:1]).then_inc(a_sq, 1)
                    if has(TB) and (not tail or head_of_tail):
                        q_feature(TB)
                        if place == "first":
                            act.wait_ge(t_kv, n)
                            for g in range(HC):
                                last = nc.scalar.activation(
                                    kv_diag[g * DH:(g + 1) * DH, :, g, :], kv_cols[g * DH:(g + 1) * DH, :, :],
                                    ACT.Copy)
                            last.then_inc(a_kv, TB)
                    if has(TB + 1):
                        act.wait_ge(d_o, n - TB)
                        if has(0):
                            act.wait_ge(a_sq, n + 1)
                        nc.scalar.activation(squares[:, :], o_raw[:, :], ACT.Square,
                                             accum_out=sum_sq[:, 2:3]).then_inc(a_so, 1)
                        act.wait_ge(a_so, n - TB)
                        nc.scalar.activation(sum_sq[:, 3:4], sum_sq[:, 2:3], ACT.Sqrt, bias=rms_eps[:, :],
                                             scale=1.0 / D).then_inc(a_ro, 1)
                    if has(TB + 2):
                        act.wait_ge(d_y, n - TB - 1)
                        act.dma_start(y_rows, y_out[:, p, :]).then_inc(y_stored[p], 16)
                    if has(0):
                        act.wait_ge(d_k, n + 1)
                        act.wait_ge(a_sq, n + 1)
                        if has(TB + 1):
                            act.wait_ge(a_so, n - TB)
                        nc.scalar.activation(squares[:, :], k_raw[:, :], ACT.Square,
                                             accum_out=sum_sq[:, 1:2]).then_inc(a_sk, 1)
                        act.wait_ge(a_sk, n + 1)
                        need(act, d_rk, n)
                        nc.scalar.activation(rms_qk[:, :], sum_sq[:, 0:2], ACT.Sqrt, bias=rms_eps[:, :],
                                             scale=1.0 / D).then_inc(a_rms, 1)
                    if head_of_tail:
                        q_feature(TB - 1)
                    if isinstance(n, int) and n in split_behind:
                        weight_high(split_behind[n])

                steps(act, step)

            @block.vector
            def _(dve):
                def weight_low(w):
                    dve.wait_ge(weight_hi, w + 1)
                    nc.vector.tensor_tensor(split[w][1], w_stage[w], f32(split[w][0]), ALU.subtract) \
                        .then_inc(weight_done, 1)

                def chunks(psum):
                    return psum[:, :].rearrange("p (c t) -> p c t", t=P)

                def times_cos(dst, src, slot):
                    return nc.vector.tensor_tensor(
                        dst[:, :].rearrange("p (g f) -> p g f", f=HF), src[:, :].rearrange("p (g f) -> p g f", f=HF),
                        cos_t[:, slot, :].unsqueeze(1).to_broadcast([P, D // HF, HF]), ALU.mult)

                def times_sin(dst, src, slot):
                    return nc.vector.tensor_tensor(
                        dst[:, :].rearrange("p (g f) -> p g f", f=DH), src[:, :].rearrange("p (g f) -> p g f", f=DH),
                        sin_t[:, slot, :].unsqueeze(1).to_broadcast([P, D // DH, DH]), ALU.mult)

                weight_low(0)

                def step(n, pair, p, slot, before, place, has):
                    tail, head_of_tail = not has(0), isinstance(n, int) and n == TILES

                    def attention(lag):
                        dve.wait_ge(t_n, n - lag + 1)
                        nums = psum_n[:, :, 0:2 * HC * EW].rearrange("p b (h e) -> p b h e", e=EW)
                        den_v = den[:, :, :].rearrange("p s (b h) -> p s b h", b=2)
                        nc.vector.tensor_scalar(den_v[:, 0], nums[:, :, :, DH],
                                                eps_q[:, bass.ds(before if lag == TB + 1 else slot, 1)], None,
                                                ALU.add).then_inc(d_de, 1)
                        dve.wait_ge(d_de, n - lag + 1)
                        nc.vector.reciprocal(den[:, 1, :], den[:, 0, :]).then_inc(d_dr, 1)
                        dve.wait_ge(d_dr, n - lag + 1)
                        need(dve, t_a, n - lag)
                        for b in (0, 1):
                            last = nc.vector.tensor_tensor(
                                attn[:, b * D // 2:(b + 1) * D // 2].rearrange("p (h d) -> p h d", d=DH),
                                nums[:, b, :, 0:DH], den_v[:, 1, b].unsqueeze(2).to_broadcast([P, HEADS // 2, DH]),
                                ALU.mult)
                        last.then_inc(d_at, 1)

                    if has(TB + 1) and (not tail or head_of_tail):
                        attention(TB + 1)
                    if has(0):
                        dve.wait_ge(a_x, n + 1)
                        nc.vector.tensor_tensor(xT_lo[:, p], xT_in[:, p], f32(xT_hi[:, p]), ALU.subtract) \
                            .then_inc(d_x, 1)
                    if isinstance(n, int) and n == 0:
                        weight_low(1)
                        dve.wait_ge(const_in, 16 * CONSTS)
                        for s in (0, 1):
                            dve.wait_ge(y_stored[s], 16)
                    if has(1):
                        dve.wait_ge(a_rms, n)
                        need(dve, a_v, n - 1)
                        nc.vector.tensor_scalar(eps_q[:, bass.ds(before, 1)], rms_qk[:, 0:1], EPS_LIN, None, ALU.mult)
                        nc.vector.reciprocal(inv_rms_k[:, :], rms_qk[:, 1:2]).then_inc(d_rk, 1)
                        dve.wait_ge(g_kg, n)
                        need(dve, g_kr, n - 1)
                        times_cos(k_cos, k_g, before)
                        times_sin(k_sin, k_g, before).then_inc(d_kp, 1)
                        dve.wait_ge(t_v, n)
                        nc.vector.tensor_tensor(v_raw[:, :], psum_v[:, :], bias_qkv[:, 2 * D:3 * D], ALU.add) \
                            .then_inc(d_v, 1)
                    if has(TB + 1):
                        dve.wait_ge(a_a, n - TB)
                        nc.vector.tensor_tensor(aT_lo[:, :, :], chunks(psum_t), f32(aT_hi[:, :, :]), ALU.subtract) \
                            .then_inc(d_a, 1)
                    if tail and not head_of_tail and has(TB):
                        attention(TB)
                    if has(TB + 2):
                        dve.wait_ge(g_h, n - TB - 1)
                        nc.vector.bn_stats(stats[:, :], h_sum[:, :]).then_inc(d_st, 1)
                        dve.wait_ge(consts_set, 1)
                        dve.wait_ge(d_st, n - TB - 1)
                        nc.vector.bn_aggr(mean_var[:, :], stats[:, :]).then_inc(d_mv, 1)
                    if has(0):
                        dve.wait_ge(t_q, n + 1)
                        need(dve, a_sq, n)
                        need(dve, g_qg, n)
                        nc.vector.tensor_tensor(q_raw[:, :], psum_q[:, :], bias_qkv[:, 0:D], ALU.add) \
                            .then_inc(d_q, 1)
                    if has(TB + 2):
                        dve.wait_ge(a_std, n - TB - 1)
                        nc.vector.reciprocal(inv_std[:, :], std_h[:, :]).then_inc(d_is, 1)
                        dve.wait_ge(d_is, n - TB - 1)
                        dve.wait_ge(y_stored[p], 16 * pair - 16 * (TB // 2))
                        nc.vector.tensor_scalar(y_out[:, p, :], h_sum[:, :], mean_var[:, 0:1], inv_std[:, :],
                                                ALU.subtract, ALU.mult).then_inc(d_y, 1)
                    if has(0):
                        dve.wait_ge(g_qg, n + 1)
                        need(dve, g_qr, n)
                        times_cos(q_cos, q_g, slot)
                    if has(TB + 1):
                        dve.wait_ge(t_o, n - TB)
                        need(dve, a_so, n - TB - 1)
                        nc.vector.tensor_tensor(o_raw[:, :], psum_o[:, :], bias_o[:, :], ALU.add).then_inc(d_o, 1)
                    if has(0):
                        times_sin(q_sin, q_g, slot).then_inc(d_qp, 1)
                    if has(TB + 1):
                        dve.wait_ge(a_ro, n - TB)
                        nc.vector.reciprocal(inv_rms_o[:, :], sum_sq[:, 3:4]).then_inc(d_ro, 1)
                        dve.wait_ge(d_ro, n - TB)
                        need(dve, g_h, n - TB - 1)
                        nc.vector.scalar_tensor_tensor(out=h_sum[:, :], in0=o_raw[:, :], scalar=inv_rms_o[:, :],
                                                       in1=gain_o[:, :], op0=ALU.mult, op1=ALU.mult) \
                            .then_inc(d_on, 1)
                    if has(0):
                        dve.wait_ge(t_k, n + 1)
                        need(dve, a_sk, n)
                        need(dve, g_kg, n)
                        nc.vector.tensor_tensor(k_raw[:, :], psum_k[:, :], bias_qkv[:, D:2 * D], ALU.add) \
                            .then_inc(d_k, 1)
                    if head_of_tail:
                        attention(TB)
                    if isinstance(n, int) and n in split_behind:
                        weight_low(split_behind[n])

                steps(dve, step)

            @block.gpsimd
            def _(pool):
                pool.memset(rms_eps[:, :], RMS_EPS)
                pool.memset(ln_eps[:, :], LN_EPS)
                pool.memset(ones[:, :], 1.0)
                pool.memset(kv_diag[:, :, :, :], 0.0).then_inc(consts_set, 1)
                pool.wait_ge(const_in, 16 * CONSTS)
                pool.wait_ge(weight_done, 2)

                def add_parts(dst, cos_part, sin_part):
                    halves = [t.rearrange("p (h s f) -> p h s f", s=2, f=HF) for t in (dst, cos_part, sin_part)]
                    for s in (0, 1):
                        last = nc.gpsimd.tensor_tensor(halves[0][:, :, s], halves[1][:, :, s],
                                                       halves[2][:, :, 1 - s], ALU.add)
                    return last

                def step(n, pair, p, slot, before, place, has):
                    if has(1):
                        pool.wait_ge(d_kp, n)
                        need(pool, a_kf, n - 1)
                        add_parts(k_rot[:, :], k_cos[:, :], k_sin[:, :]).then_inc(g_kr, 1)
                    if has(0):
                        pool.wait_ge(d_q, n + 1)
                        need(pool, d_qp, n)
                        nc.gpsimd.tensor_tensor(q_g[:, :], q_raw[:, :], gain_qk[:, 0:D], ALU.mult).then_inc(g_qg, 1)
                        pool.wait_ge(d_qp, n + 1)
                        if has(TB):
                            pool.wait_ge(q_fetched[p], 16 * pair - 16 * (TB // 2) + 16)
                        add_parts(q_ring[:, slot, :], q_cos[:, :], q_sin[:, :]).then_inc(g_qr, 1)
                    if has(TB + 1):
                        pool.wait_ge(d_on, n - TB)
                        pool.wait_ge(res_loaded, 16 * n - 16 * TB)
                        need(pool, d_y, n - TB - 1)
                        nc.gpsimd.tensor_tensor(h_sum[:, :], h_sum[:, :], x_res[:, :], ALU.add).then_inc(g_h, 1)
                    if has(0):
                        pool.wait_ge(d_k, n + 1)
                        need(pool, d_kp, n)
                        nc.gpsimd.tensor_tensor(k_g[:, :], k_raw[:, :], gain_qk[:, D:2 * D], ALU.mult).then_inc(g_kg, 1)

                steps(pool, step)

        with ExitStack() as pb:
            psum_y = pb.enter_context(nc.psum_tensor("psum_y", [P, 2, BLK], F32))
            psum_u = pb.enter_context(nc.psum_tensor("psum_u", [P, 2, BLK], F32))
            psum_r = pb.enter_context(nc.psum_tensor("psum_r", [P, 2, D], F32))
            psum_w = pb.enter_context(nc.psum_tensor("psum_w", [P, 2, D], F32))
            y_chunks = [psum_y[:, 0, :], psum_y[:, 1, :], psum_u[:, 0, :], psum_u[:, 1, :]]
            yT = sb(pb, "yT", [P, 2, KC, BLK + 1])
            diff = sb(pb, "diff", [P, KC, BLK])
            mix = sb(pb, "mix", [P, 2, BLK])
            xk_hi = sb(pb, "xk_hi", [P, KC, BLK], F32R)
            xk_lo = sb(pb, "xk_lo", [P, KC, BLK], F32R)
            xr_hi = sb(pb, "xr_hi", [P, KC, BLK], F32R)
            xr_lo = sb(pb, "xr_lo", [P, KC, BLK], F32R)
            relu_u = sb(pb, "relu_u", [P, 2, BLK])
            act_u = sb(pb, "act_u", [P, 2, BLK])
            uT_hi = sb(pb, "uT_hi", [P, KC, BLK], F32R)
            uT_lo = sb(pb, "uT_lo", [P, KC, BLK], F32R)
            gate = sb(pb, "gate", [P, BT, D])
            z = sb(pb, "z", [P, BT, D])
            z_stats = sb(pb, "z_stats", [P, BT, 6])
            z_mv = sb(pb, "z_mv", [P, BT, 2])
            z_std = sb(pb, "z_std", [P, BT])
            z_inv = sb(pb, "z_inv", [P, BT])
            z_out = sb(pb, "z_out", [P, BT, D])

            out_stored = sem("out_stored")
            zero_set = sem("zero_set")
            t_y = sem("t_y")
            t_u = sem("t_u")
            t_r = sem("t_r")
            t_w = sem("t_w")
            a_y = sem("a_y")
            a_c = sem("a_c")
            a_mh = sem("a_mh")
            a_ru = sem("a_ru")
            a_uh = sem("a_uh")
            a_zs = sem("a_zs")
            a_g = sem("a_g")
            d_m = sem("d_m")
            d_ml = sem("d_ml")
            d_z = sem("d_z")
            d_zs = sem("d_zs")
            d_zm = sem("d_zm")
            d_ul = sem("d_ul")
            d_zi = sem("d_zi")
            d_zo = sem("d_zo")
            g_d = sem("g_d")
            g_z = sem("g_z")
            g_u = sem("g_u")

            def blocks(eng, step):
                for s in (0, 1):
                    step(s, 0, s, s == 0)
                with eng.Fori(1, BLOCKS // BPB) as b:
                    for s in (0, 1):
                        step(2 * b + s, b, s, False)
                step(BLOCKS, BLOCKS // BPB, 0, False)

            block = pb.enter_context(nc.Block())

            @block.sync
            def _(sp):
                def tokens(dram, m):
                    return block_rows(dram, m if isinstance(m, int) else sp.snap(m * BLK))

                def step(m, b, s, first):
                    more = not (isinstance(m, int) and m == BLOCKS)
                    done = not (isinstance(m, int) and m < 2)
                    load = more and not (isinstance(m, int) and m < 2)
                    y_rows = tokens(y_mid, m) if load else None
                    out_rows = tokens(out, m - 2) if done else None
                    used, before = (v if isinstance(v, int) else sp.snap(v) for v in (BT * m - BT, m - 1))
                    if load:
                        sp.wait_ge(g_z, used)
                        sp.dma_start(y_in[:, s], y_rows).then_inc(y_loaded[s], 16)
                    if done:
                        sp.wait_ge(d_zo, before)
                        sp.dma_start(out_rows, z_out[:, :, :]).then_inc(out_stored, 16)

                for p in (0, 1):
                    sp.wait_ge(y_stored[p], 16 * (TILES // 2) + 16)
                blocks(sp, step)
                sp.wait_ge(d_zo, BLOCKS)
                sp.dma_start(tokens(out, BLOCKS - 1), z_out[:, :, :]).then_inc(out_stored, 16)
                sp.wait_ge(out_stored, 16 * BLOCKS)

            @block.tensor
            def _(pe):
                def product(psum, lhs_hi, lhs_lo, rhs_hi, rhs_lo):
                    for c in range(KC):
                        nc.tensor.matmul(psum, lhs_hi(c), rhs_hi(c), start=(c == 0), stop=False)
                        nc.tensor.matmul(psum, lhs_hi(c), rhs_lo(c), start=False, stop=False)
                        last = nc.tensor.matmul(psum, lhs_lo(c), rhs_hi(c), start=False, stop=(c == KC - 1))
                    return last

                def step(m, b, s, first):
                    more = not (isinstance(m, int) and m == BLOCKS)
                    if more:
                        pe.wait_ge(y_loaded[s], 16 * b + 16)
                        for c in range(KC):
                            if c < 2:
                                need(pe, a_y, KC * m - KC + c + 1)
                            else:
                                need(pe, a_ru, KC * m - KC + c + 1)
                            for t in range(BT):
                                last = nc.tensor.transpose(y_chunks[c][:, t * P:(t + 1) * P],
                                                           y_in[:, s, t, c * P:(c + 1) * P], ident[:, :])
                            last.then_inc(t_y, 1)
                    if not first:
                        pe.wait_ge(d_ul, KC * m)
                        for t in range(BT):
                            need(pe, d_z, BT * m - BT + t - 1)
                            tok = slice(t * P, (t + 1) * P)
                            product(psum_w[:, t % 2, :], lambda c: uT_hi[:, c, tok], lambda c: uT_lo[:, c, tok],
                                    lambda c: wb_hi[:, WVF, c, :], lambda c: wb_lo[:, WVF, c, :]).then_inc(t_w, 1)
                    if more:
                        pe.wait_ge(d_ml, 2 * KC * m + KC)
                        for o in range(KC):
                            need(pe, a_ru, KC * m + o - 1)
                            feat = slice(o * P, (o + 1) * P)
                            product(psum_u[:, o % 2, :], lambda c: wb_hi[:, WKF, c, feat],
                                    lambda c: wb_lo[:, WKF, c, feat], lambda c: xk_hi[:, c, :],
                                    lambda c: xk_lo[:, c, :]).then_inc(t_u, 1)
                        pe.wait_ge(d_ml, 2 * KC * m + 2 * KC)
                        for t in range(BT):
                            need(pe, a_g, BT * m + t - 1)
                            tok = slice(t * P, (t + 1) * P)
                            product(psum_r[:, t % 2, :], lambda c: xr_hi[:, c, tok], lambda c: xr_lo[:, c, tok],
                                    lambda c: wb_hi[:, WR, c, :], lambda c: wb_lo[:, WR, c, :]).then_inc(t_r, 1)

                blocks(pe, step)

            @block.scalar
            def _(act):
                def step(m, b, s, first):
                    more = not (isinstance(m, int) and m == BLOCKS)
                    if more:
                        need(act, d_m, 2 * KC * m - 2 * KC)
                        if s == 1:
                            act.wait_ge(a_y, KC * m)
                            nc.scalar.activation(yT[:, 1, :, 0], yT[:, 0, :, BLK], ACT.Copy).then_inc(a_c, 1)
                        for c in range(KC):
                            act.wait_ge(t_y, KC * m + c + 1)
                            nc.scalar.activation(yT[:, s, c, 1:BLK + 1], y_chunks[c], ACT.Copy) \
                                .then_inc(a_y, 1)
                        for i in range(2 * KC):
                            c, hi = i % KC, (xk_hi, xr_hi)[i // KC]
                            if i == 0:
                                need(act, t_u, KC * m)
                            if i == KC:
                                need(act, t_r, BT * m)
                            act.wait_ge(d_m, 2 * KC * m + i + 1)
                            nc.scalar.activation(hi[:, c, :], mix[:, i % 2, :], ACT.Copy).then_inc(a_mh, 1)
                        need(act, t_w, BT * m)
                        for o in range(KC):
                            act.wait_ge(t_u, KC * m + o + 1)
                            need(act, g_u, KC * m + o - 1)
                            nc.scalar.activation(relu_u[:, o % 2, :], psum_u[:, o % 2, :], ACT.Relu) \
                                .then_inc(a_ru, 1)
                            act.wait_ge(a_ru, KC * m + o + 1)
                            nc.scalar.activation(uT_hi[:, o, :], relu_u[:, o % 2, :], ACT.Square).then_inc(a_uh, 1)
                    if not first:
                        act.wait_ge(d_zm, BT * m)
                        nc.scalar.activation(z_std[:, :], z_mv[:, :, 1], ACT.Sqrt, bias=ln_eps[:, :]) \
                            .then_inc(a_zs, 1)
                    if more:
                        need(act, d_z, BT * m)
                        for t in range(BT):
                            act.wait_ge(t_r, BT * m + t + 1)
                            nc.scalar.activation(gate[:, t, :], psum_r[:, t % 2, :], ACT.Sigmoid).then_inc(a_g, 1)

                blocks(act, step)

            @block.vector
            def _(dve):
                dve.wait_ge(zero_set, 1)

                def step(m, b, s, first):
                    more = not (isinstance(m, int) and m == BLOCKS)

                    def low(i):
                        c, hi, lo = i % KC, (xk_hi, xr_hi)[i // KC], (xk_lo, xr_lo)[i // KC]
                        dve.wait_ge(a_mh, 2 * KC * m + i + 1)
                        nc.vector.tensor_tensor(lo[:, c, :], mix[:, i % 2, :], f32(hi[:, c, :]), ALU.subtract) \
                            .then_inc(d_ml, 1)

                    for i in range(2 * KC):
                        c = i % KC
                        if more:
                            if i < KC:
                                dve.wait_ge(g_d, KC * m + c + 1)
                            if i >= 2:
                                dve.wait_ge(d_ml, 2 * KC * m + i - 1)
                            nc.vector.scalar_tensor_tensor(
                                out=mix[:, i % 2, :], in0=diff[:, c, :], scalar=mu[:, 1 - i // KC, c:c + 1],
                                in1=yT[:, s, c, 0:BLK], op0=ALU.mult, op1=ALU.add).then_inc(d_m, 1)
                            if i:
                                low(i - 1)
                        if not first and i % 2:
                            t = i // 2
                            dve.wait_ge(t_w, BT * m - BT + t + 1)
                            if t == 0:
                                dve.wait_ge(a_g, BT * m)
                                need(dve, d_zo, m - 1)
                            nc.vector.tensor_tensor(z[:, t, :], psum_w[:, t % 2, :], gate[:, t, :], ALU.mult) \
                                .then_inc(d_z, 1)
                    if more:
                        low(2 * KC - 1)
                    if not first:
                        for t in range(BT):
                            dve.wait_ge(g_z, BT * m - BT + t + 1)
                            nc.vector.bn_stats(z_stats[:, t, :], z[:, t, :]).then_inc(d_zs, 1)
                        for t in range(BT):
                            dve.wait_ge(zero_set, 1)
                            dve.wait_ge(d_zs, BT * m - BT + t + 1)
                            nc.vector.bn_aggr(z_mv[:, t, :], z_stats[:, t, :]).then_inc(d_zm, 1)
                    if more:
                        for o in range(KC):
                            dve.wait_ge(a_uh, KC * m + o + 1)
                            dve.wait_ge(g_u, KC * m + o + 1)
                            nc.vector.tensor_tensor(uT_lo[:, o, :], act_u[:, o % 2, :], f32(uT_hi[:, o, :]),
                                                    ALU.subtract).then_inc(d_ul, 1)
                    if not first:
                        dve.wait_ge(a_zs, m)
                        nc.vector.reciprocal(z_inv[:, :], z_std[:, :]).then_inc(d_zi, 1)
                        dve.wait_ge(d_zi, m)
                        if not (isinstance(m, int) and m == 1):
                            dve.wait_ge(out_stored, 16 * m - 16)
                        for t in range(BT):
                            last = nc.vector.tensor_scalar(z_out[:, t, :], z[:, t, :], z_mv[:, t, 0:1],
                                                           z_inv[:, t:t + 1], ALU.subtract, ALU.mult)
                        last.then_inc(d_zo, 1)

                blocks(dve, step)

            @block.gpsimd
            def _(pool):
                pool.memset(yT[:, 0, :, 0:1], 0.0).then_inc(zero_set, 1)
                pool.wait_ge(zero_set, 1)

                def step(m, b, s, first):
                    more = not (isinstance(m, int) and m == BLOCKS)
                    if more:
                        need(pool, d_m, 2 * KC * m)
                        if s == 1:
                            pool.wait_ge(a_c, b + 1)
                        for c in range(KC):
                            pool.wait_ge(a_y, KC * m + c + 1)
                            nc.gpsimd.tensor_tensor(diff[:, c, :], yT[:, s, c, 1:BLK + 1], yT[:, s, c, 0:BLK],
                                                    ALU.subtract).then_inc(g_d, 1)
                    if not first:
                        for t in range(BT):
                            pool.wait_ge(d_z, BT * m - BT + t + 1)
                            nc.gpsimd.tensor_tensor(z[:, t, :], z[:, t, :], y_in[:, 1 - s, t, :], ALU.add) \
                                .then_inc(g_z, 1)
                    if more:
                        for o in range(KC):
                            pool.wait_ge(a_ru, KC * m + o + 1)
                            need(pool, d_ul, KC * m + o - 1)
                            nc.gpsimd.tensor_tensor(act_u[:, o % 2, :], relu_u[:, o % 2, :], relu_u[:, o % 2, :],
                                                    ALU.mult).then_inc(g_u, 1)

                blocks(pool, step)


_FROM_REFERENCE = {"x": "L0_attn_x", "w_r": "L0_ffn_W_r", "w_k": "L0_ffn_W_k", "w_v": "L0_ffn_W_v",
                   "mu_r": "L0_ffn_mu_r", "mu_k": "L0_ffn_mu_k"}


def kernel(**inputs):
    import concourse.bacc as bacc
    from concourse.bass_utils import run_bass_kernel_spmd

    given = {name: np.asarray(a) for name, a in inputs.items()}
    x = given["L0_attn_x"]
    B, L, D = x.shape
    DH = D // HEADS
    order = np.arange(D).reshape(HEADS, DH // 2, 2).transpose(0, 2, 1).reshape(D)
    order_qkv = np.concatenate([order, D + order, 2 * D + np.arange(D)])
    inv_freq = (1.0 / np.float32(10000.0) ** (np.arange(0, DH, 2, dtype=np.float32) / np.float32(DH))).astype(np.float32)
    angles = np.outer(np.arange(L, dtype=np.float32), inv_freq).astype(np.float32)
    cos, sin = np.cos(angles), np.sin(angles)

    def laid(a):
        return np.ascontiguousarray(a)

    arrays = {
        "x": laid(x.reshape(B * L, D)),
        "x_T": laid(x.reshape(B * L // P, P, D // P, P).transpose(0, 3, 2, 1)),
        "w_qkv": laid(given["L0_attn_Wqkv"][order_qkv].T),
        "b_qkv": laid(given["L0_attn_bqkv"][order_qkv]),
        "g_qk": laid(np.concatenate([given["L0_attn_gq"][order], given["L0_attn_gk"][order]])),
        "w_out": laid(given["L0_attn_Wout"].T),
        "b_out": laid(given["L0_attn_bout"]),
        "g_out": laid(given["L0_attn_gout"]),
        "w_r": laid(given["L0_ffn_W_r"].T),
        "w_k": laid(given["L0_ffn_W_k"].T),
        "w_v": laid(given["L0_ffn_W_v"].T),
        "mu_r": laid(given["L0_ffn_mu_r"]),
        "mu_k": laid(given["L0_ffn_mu_k"]),
        "rope_cos": laid(cos),
        "rope_sin": laid(np.concatenate([sin, -sin], axis=1)),
        "identity": np.eye(P, dtype=np.float32),
    }
    nc = bacc.Bacc("TRN2", target_bir_lowering=False, num_devices=1, dynamic_dma_scratch_size=1024)
    args = {n: nc.dram_tensor(n, a.shape, mybir.dt.from_np(a.dtype), kind="ExternalInput").ap() for n, a in arrays.items()}
    out = nc.dram_tensor("out", (B * L, D), F32, kind="ExternalOutput").ap()
    y_mid = nc.dram_tensor("y_mid", (B * L, D), F32, kind="Internal").ap()
    postnorm_layer(nc, **args, out=out, y_mid=y_mid)
    r = run_bass_kernel_spmd(nc, [arrays], core_ids=[0])
    return r.results[0]["out"].reshape(B, L, D)
```

```python
from contextlib import ExitStack

import numpy as np

import concourse.bass as bass
from concourse import mybir

ALU = mybir.AluOpType
ACT = mybir.ActivationFunctionType
F32 = mybir.dt.float32
F32R = mybir.dt.float32r

P = 128
HEADS = 16
RMS_EPS = 1.1920929e-07
EPS_LIN = 1e-06
LN_EPS = 1e-05


def need(eng, sem, count):
    if not isinstance(count, int) or count > 0:
        eng.wait_ge(sem, count)


def f32(ap):
    return ap.bitcast(F32)


def postnorm_layer(nc, x, x_T, w_qkv, b_qkv, g_qk, w_out, b_out, g_out, w_ffn, mu_r, mu_k,
                   rope_cos, rope_sin, identity, out, y_mid):
    TOKENS, D = x.shape
    L = rope_cos.shape[0]
    KC = D // P
    DH = D // HEADS
    HF = DH // 2
    HC = P // DH
    NC = HEADS // HC
    EW = DH + 1
    TILES = TOKENS // P
    TB = L // P
    assert TB % 2 == 0 and TILES % TB == 0
    BT = 4
    BLK = BT * P
    BLOCKS = TOKENS // BLK
    BPB = L // BLK
    assert BPB == 2

    ctx = ExitStack()

    def sb(scope, name, shape, dt=F32):
        return scope.enter_context(nc.sbuf_tensor(name, shape, dt))

    def sem(name):
        return ctx.enter_context(nc.semaphore(name))

    with ctx:
        WR, WKF, WVF = range(3)
        wb_hi = sb(ctx, "wb_hi", [P, 3, KC, D], F32R)
        wb_lo = sb(ctx, "wb_lo", [P, 3, KC, D], F32R)
        ln_eps = sb(ctx, "ln_eps", [P, 1])
        y_in = sb(ctx, "y_in", [P, 2, BT, D])
        y_loaded = [sem("y_loaded0"), sem("y_loaded1")]
        y_out = sb(ctx, "y_out", [P, 2, D])
        y_stored = [sem("y_stored0"), sem("y_stored1")]

        def block_rows(dram, m):
            return dram[bass.ds(m * BLK if isinstance(m, int) else m, BLK), :].rearrange("(t p) d -> p t d", p=P)

        ident = sb(ctx, "ident", [P, P])
        mu = sb(ctx, "mu", [P, 2, KC])
        chunk_in = [[sem(f"chunk_in{w}{c}") for c in range(KC)] for w in range(3)]
        chunk_hi = sem("chunk_hi")
        chunk_done = sem("chunk_done")
        pair_in = [sem("pair_in0"), sem("pair_in1")]
        late_hi = sem("late_hi")
        late_done = sem("late_done")
        LATE = 4 * KC
        ident_in = sem("ident_in")
        bias_in = sem("bias_in")
        const_in = sem("const_in")

        early = sb(ctx, "early", [P, 2 * KC * P + 9 * D + 2 * D + 2 * HEADS * EW + 5 * D + TB * 3 * HF + (TB + 2) * D])
        early_r = sb(ctx, "early_r", [P, 6 * KC * D + 4 * KC * P], F32R)

        def cutter():
            used = {False: 0, True: 0}

            def cut(shape, dt=F32):
                rounded = dt is F32R
                first, used[rounded] = used[rounded], used[rounded] + int(np.prod(shape[1:]))
                whole = early_r if rounded else early
                assert used[rounded] <= whole.shape[1]
                piece = whole[:, first:used[rounded]]
                names = "abcd"[:len(shape) - 1]
                if len(names) > 1:
                    piece = piece.rearrange(f"p ({' '.join(names)}) -> p {' '.join(names)}",
                                            **dict(zip(names, shape[1:])))
                return piece

            return cut

        def bank(name, count=1):
            return ctx.enter_context(nc.psum_tensor(name, [P, D] if count == 1 else [P, count, D], F32))

        WQ, WK, WV, WO = range(4)
        cut = cutter()
        wa_hi = cut([P, 3, KC, D], F32R)
        wa_lo = cut([P, 3, KC, D], F32R)
        xT_in = cut([P, 2, KC, P])
        xT_hi = cut([P, 2, KC, P], F32R)
        xT_lo = cut([P, 2, KC, P], F32R)
        q_raw, k_raw, v_raw = (cut([P, D]) for _ in range(3))
        q_g, k_g = (cut([P, D]) for _ in range(2))
        q_cos, q_sin, k_cos, k_sin = (cut([P, D]) for _ in range(4))
        k_rot, k_feat = (cut([P, D]) for _ in range(2))
        v_ext = cut([P, HEADS, EW])
        bias_qkv = cut([P, 3 * D])
        gain_qk = cut([P, 2 * D])
        cos_t = cut([P, TB, HF])
        sin_t = cut([P, TB, DH])
        q_ring = cut([P, TB, D])
        q_tile = cut([P, 2, D])
        kv_diag = cut([P, NC, HC, EW])
        psum_q, psum_k, psum_v, psum_o, psum_t, psum_kv = (
            bank(f"psum_{name}") for name in ("q", "k", "v", "o", "t", "kv"))
        psum_n = bank("psum_n", 2)
        kv_cols = psum_kv[:, 0:NC * EW].rearrange("p (c e) -> p c e", e=EW)

        wo_hi = sb(ctx, "wo_hi", [P, KC, D], F32R)
        wo_lo = sb(ctx, "wo_lo", [P, KC, D], F32R)
        rms_eps = sb(ctx, "rms_eps", [P, 1])
        bias_o = sb(ctx, "bias_o", [P, D])
        gain_o = sb(ctx, "gain_o", [P, D])
        ones = sb(ctx, "ones", [P, HEADS])
        x_res = sb(ctx, "x_res", [P, D])
        squares = sb(ctx, "squares", [P, D])
        sum_sq = sb(ctx, "sum_sq", [P, 4])
        rms_qk = sb(ctx, "rms_qk", [P, 2])
        inv_rms_k = sb(ctx, "inv_rms_k", [P, 1])
        eps_q = sb(ctx, "eps_q", [P, TB])
        qT_feat = sb(ctx, "qT_feat", [P, NC, P])
        den = sb(ctx, "den", [P, 2, HEADS])
        attn = sb(ctx, "attn", [P, D])
        aT_hi = sb(ctx, "aT_hi", [P, KC, P], F32R)
        aT_lo = sb(ctx, "aT_lo", [P, KC, P], F32R)
        o_raw = sb(ctx, "o_raw", [P, D])
        h_sum = sb(ctx, "h_sum", [P, D])
        inv_rms_o = sb(ctx, "inv_rms_o", [P, 1])
        stats = sb(ctx, "stats", [P, 6])
        mean_var = sb(ctx, "mean_var", [P, 2])
        std_h = sb(ctx, "std_h", [P, 1])
        inv_std = sb(ctx, "inv_std", [P, 1])
        w_stage = [q_ring[:, 0:KC, :], q_ring[:, KC:2 * KC, :], y_in[:, 0]]
        assert KC == BT and LATE == 2 * TB and TB <= 2 * KC
        CONSTS = 5

        x_loaded = [sem("x_loaded0"), sem("x_loaded1")]
        res_loaded = sem("res_loaded")
        q_fetched = [sem("q_fetched0"), sem("q_fetched1")]
        consts_set = sem("consts_set")
        t_v = sem("t_v")
        t_a = sem("t_a")
        t_q = sem("t_q")
        t_o = sem("t_o")
        t_qT = sem("t_qT")
        t_kv = sem("t_kv")
        t_k = sem("t_k")
        t_n = sem("t_n")
        a_x = sem("a_x")
        a_v = sem("a_v")
        a_kf = sem("a_kf")
        a_a = sem("a_a")
        a_sq = sem("a_sq")
        a_qT = sem("a_qT")
        a_kv = sem("a_kv")
        a_so = sem("a_so")
        a_ro = sem("a_ro")
        a_sk = sem("a_sk")
        a_rms = sem("a_rms")
        a_std = sem("a_std")
        d_x = sem("d_x")
        d_v = sem("d_v")
        d_a = sem("d_a")
        d_q = sem("d_q")
        d_o = sem("d_o")
        d_qp = sem("d_qp")
        d_ro = sem("d_ro")
        d_on = sem("d_on")
        d_k = sem("d_k")
        d_de = sem("d_de")
        d_dr = sem("d_dr")
        d_at = sem("d_at")
        d_st = sem("d_st")
        d_mv = sem("d_mv")
        d_rk = sem("d_rk")
        d_is = sem("d_is")
        d_y = sem("d_y")
        d_kp = sem("d_kp")
        g_qg = sem("g_qg")
        g_qr = sem("g_qr")
        g_h = sem("g_h")
        g_kg = sem("g_kg")
        g_kr = sem("g_kr")

        def steps(eng, step):
            half = TB // 2

            def static(n):
                t = n % TB
                step(n, n // 2, n % 2, t, (t - 1) % TB, ("first", "second")[t] if t < 2 else "inner",
                     lambda lag: 0 <= n - lag < TILES)

            def head(batch):
                for p, place in ((0, "first"), (1, "second")):
                    step(2 * half * batch + p, half * batch, p, p, (p - 1) % TB, place, lambda lag: True)

            def inner(batch, has, pairs=half):
                with eng.Fori(1, pairs) as r:
                    for p in (0, 1):
                        step((TB * batch + p) + 2 * r, half * batch + r, p, 2 * r + p, 2 * r + (p - 1),
                             "inner", has)

            static(0)
            static(1)
            inner(0, lambda lag: lag < TB)
            static(TB)
            static(TB + 1)
            inner(1, lambda lag: True)
            with eng.Fori(2, TILES // TB) as batch:
                head(batch)
                inner(batch, lambda lag: True)
            static(TILES)
            static(TILES + 1)
            inner(TILES // TB, lambda lag: lag >= TB - 2, half - 1)
            for n in range(TILES + TB - 2, TILES + TB + 2):
                static(n)

        def late_chunks(n, p, pair):
            def entry(t, half, i, hi, lo):
                return (pair_in[half], 16 if isinstance(t, int) else 16 * pair + 16, 2 * t + i + 1,
                        y_in[:, 1, 2 * half + i], hi, lo)

            if is_step(n, 1):
                return [[entry(t, t, i, wo_hi[:, 2 * t + i], wo_lo[:, 2 * t + i]) for i in (0, 1)]
                        for t in (0, 1)]
            flat_hi, flat_lo = (w.rearrange("p w c d -> p (w c) d") for w in (wb_hi, wb_lo))
            return [[entry(n, p, i, flat_hi[:, 2 * n + (i - 4)], flat_lo[:, 2 * n + (i - 4)])]
                    for i in (0, 1)]

        def is_step(n, at):
            return isinstance(n, int) and n == at

        def x_ahead(has):
            return has(0) and not has(TB)

        def x_at_start(n, has):
            return is_step(n, 0) or not x_ahead(has) and not is_step(n, TB)

        def fetch_lags(n, has):
            if is_step(n, TILES):
                return TB, TB - 1, TB - 2
            lag = TB if has(0) else TB - 2
            return (lag,) if has(lag) else ()

        def parity(p, lag):
            return p if lag % 2 == 0 else 1 - p

        psum_u, psum_r, psum_w = [psum_kv, psum_q], [psum_n[:, 0], psum_n[:, 1]], [psum_o, psum_t]
        y_chunks = [psum_k, psum_v] + psum_u
        y_chunks_free = [d_k, d_v, a_kv, a_qT]
        cut = cutter()
        yT = cut([P, 2, KC, BLK + 1])
        diff = cut([P, KC, BLK])
        mix = cut([P, 2, BLK])
        xk_hi = cut([P, KC, BLK], F32R)
        xk_lo = cut([P, KC, BLK], F32R)
        xr_hi = cut([P, KC, BLK], F32R)
        xr_lo = cut([P, KC, BLK], F32R)
        relu_u = cut([P, 2, BLK])
        act_u = cut([P, 2, BLK])
        uT_hi = cut([P, KC, BLK], F32R)
        uT_lo = cut([P, KC, BLK], F32R)
        gate = cut([P, BT, D])
        z = cut([P, BT, D])
        z_stats = cut([P, BT, 6])
        z_mv = cut([P, BT, 2])
        z_std = cut([P, BT])
        z_inv = cut([P, BT])
        z_out = cut([P, BT, D])

        out_stored = sem("out_stored")
        zero_set = sem("zero_set")
        t_y = sem("t_y")
        t_u = sem("t_u")
        t_r = sem("t_r")
        t_w = sem("t_w")
        a_y = sem("a_y")
        a_c = sem("a_c")
        a_mh = sem("a_mh")
        a_ru = sem("a_ru")
        a_uh = sem("a_uh")
        a_zs = sem("a_zs")
        a_g = sem("a_g")
        d_m = sem("d_m")
        d_ml = sem("d_ml")
        d_z = sem("d_z")
        d_zs = sem("d_zs")
        d_zm = sem("d_zm")
        d_ul = sem("d_ul")
        d_zi = sem("d_zi")
        d_zo = sem("d_zo")
        g_d = sem("g_d")
        g_z = sem("g_z")
        g_u = sem("g_u")

        carriers = [TILES + 1] + [TILES + TB + i for i in (-2, -1, 0, 1)]

        def y_chunk_in(n):
            return [c for c in range(KC) if is_step(n, carriers[c])]

        def xk_chunk_in(n):
            return [c for c in range(KC) if is_step(n, carriers[c + 1])]

        def blocks(eng, step):
            for s in (0, 1):
                step(s, 0, s, s == 0)
            with eng.Fori(1, BLOCKS // BPB) as b:
                for s in (0, 1):
                    step(2 * b + s, b, s, False)
            step(BLOCKS, BLOCKS // BPB, 0, False)

        block = ctx.enter_context(nc.Block())

        @block.sync
        def _(sp):
            def load_pair(half, dram_rows):
                sp.dma_start(y_in[:, 1, 2 * half:2 * half + 2], dram_rows.rearrange("(c p) d -> p c d", p=P)) \
                    .then_inc(pair_in[half], 16)

            def load_chunk(w, c):
                sp.dma_start(w_stage[w][:, c], w_qkv[c * P:(c + 1) * P, w * D:(w + 1) * D]).then_inc(chunk_in[w][c], 16)

            consts = ((mu[:, 0, :], mu_r.rearrange("(c p) -> p c", p=P)),
                      (mu[:, 1, :], mu_k.rearrange("(c p) -> p c", p=P)),
                      (gain_qk[:, :], g_qk.partition_broadcast(P)),
                      (cos_t[:, :, :], rope_cos.rearrange("(t p) f -> p t f", p=P)),
                      (sin_t[:, :, :], rope_sin.rearrange("(t p) f -> p t f", p=P)))
            assert len(consts) == CONSTS

            def ahead(count):
                return count if isinstance(count, int) else sp.snap(count)

            def rows(dram, first):
                return dram[bass.ds(ahead(first), P), :]

            def step(n, pair, p, slot, before, place, has):
                late_tail = not has(0) and not is_step(n, TILES)
                lead = 1 if x_ahead(has) else 0
                tile = x_T[bass.ds(ahead(n + lead), 1)].rearrange("n p c t -> (n p) c t") if has(0) else None
                ring_slots = {lag: ahead(slot + TB - lag) for lag in fetch_lags(n, has)}
                taken = {lag: ahead(n - lag - 1) for lag in fetch_lags(n, has)}
                res_rows = rows(x, n * P - (TB + 1) * P) if has(TB + 1) else None
                x_taken, m9 = ahead(n + lead - 1), ahead(n - TB - 1)
                if has(1) and x_ahead(has) and not is_step(n, 1):
                    pairs_split, pair_rows = ahead(2 * n - 2), w_ffn[bass.ds(ahead(n * 2 * P - 4 * P), 2 * P), :]
                if late_tail and has(TB + 2):
                    y_rows, stored = rows(y_mid, n * P - (TB + 2) * P), ahead(n - TB - 1)
                if is_step(n, 0):
                    sp.dma_start(xT_in[:, 0], x_T[0]).then_inc(x_loaded[0], 16)
                elif has(0) and not is_step(n, TB):
                    sp.wait_ge(d_x, x_taken)
                    sp.dma_start(xT_in[:, (p + lead) % 2], tile).then_inc(x_loaded[(p + lead) % 2], 16)
                if has(1) and x_ahead(has) and not is_step(n, 1):
                    sp.wait_ge(late_done, pairs_split)
                    load_pair(p, pair_rows)
                if is_step(n, 1):
                    for half in (0, 1):
                        load_pair(half, w_out[half * 2 * P:(half + 1) * 2 * P, :])
                    sp.dma_start(bias_o[:, :], b_out.partition_broadcast(P)).then_inc(y_stored[0], 16)
                    sp.dma_start(gain_o[:, :], g_out.partition_broadcast(P)).then_inc(y_stored[1], 16)
                if is_step(n, 0):
                    for w in range(3):
                        for c in range(KC):
                            load_chunk(w, c)
                    sp.dma_start(xT_in[:, 1], x_T[1]).then_inc(x_loaded[1], 16)
                    sp.dma_start(bias_qkv[:, :], b_qkv.partition_broadcast(P)).then_inc(bias_in, 16)
                    for dst, src in consts:
                        sp.dma_start(dst, src, allow_slow_non_contiguous=True).then_inc(const_in, 16)
                    sp.dma_start(ident[:, :], identity).then_inc(ident_in, 16)
                for lag in fetch_lags(n, has):
                    if isinstance(n, int) and n <= TB + 1:
                        sp.wait_ge(g_qr, n - TB + 1)
                    elif has(0):
                        sp.wait_ge(t_qT, taken[lag])
                    else:
                        sp.wait_ge(t_qT, taken[lag])
                    sp.dma_start(q_tile[:, parity(p, lag), :], q_ring[:, ring_slots[lag], :]) \
                        .then_inc(q_fetched[parity(p, lag)], 16)
                if has(TB + 1):
                    need(sp, g_h, m9)
                    sp.dma_start(x_res[:, :], res_rows).then_inc(res_loaded, 16)
                if late_tail and has(TB + 2):
                    sp.wait_ge(d_y, stored)
                    sp.dma_start(y_rows, y_out[:, p, :]).then_inc(y_stored[p], 16)
                if isinstance(n, int) and TILES <= n < TILES + 2:
                    for s in (0, 1):
                        sp.wait_ge(y_stored[s], 16 * (BT * (n - TILES + 1) // 2) + 16)
                    if p == 1:
                        sp.wait_ge(late_done, LATE)
                    sp.wait_ge(chunk_done, 3 * KC)
                    sp.dma_start(y_in[:, p], block_rows(y_mid, n - TILES)).then_inc(y_loaded[p], 16)

            steps(sp, step)

            def tokens(dram, m):
                return block_rows(dram, m if isinstance(m, int) else sp.snap(m * BLK))

            def mix_step(m, b, s, first):
                more = not (isinstance(m, int) and m == BLOCKS)
                done = not (isinstance(m, int) and m < 2)
                load = more and not (isinstance(m, int) and m < 2)
                y_rows = tokens(y_mid, m) if load else None
                out_rows = tokens(out, m - 2) if done else None
                used, before = (v if isinstance(v, int) else sp.snap(v) for v in (BT * m - BT, m - 1))
                if load:
                    sp.wait_ge(g_z, used)
                    sp.dma_start(y_in[:, s], y_rows).then_inc(y_loaded[s], 16)
                if done:
                    sp.wait_ge(d_zo, before)
                    sp.dma_start(out_rows, z_out[:, :, :]).then_inc(out_stored, 16)

            for p in (0, 1):
                sp.wait_ge(y_stored[p], 16 * (TILES // 2) + 16)
            blocks(sp, mix_step)
            sp.wait_ge(d_zo, BLOCKS)
            sp.dma_start(tokens(out, BLOCKS - 1), z_out[:, :, :]).then_inc(out_stored, 16)
            sp.wait_ge(out_stored, 16 * BLOCKS)

        @block.tensor
        def _(pe):
            def product(psum, lhs_hi, lhs_lo, w, chunkwise=False):
                w_hi, w_lo = (wo_hi, wo_lo) if w == WO else (wa_hi[:, w], wa_lo[:, w])
                for c in range(KC):
                    if chunkwise:
                        pe.wait_ge(chunk_done, KC * w + c + 1)
                    nc.tensor.matmul(psum, lhs_hi[:, c, :], w_hi[:, c, :], start=(c == 0), stop=False)
                    nc.tensor.matmul(psum, lhs_hi[:, c, :], w_lo[:, c, :], start=False, stop=False)
                    last = nc.tensor.matmul(psum, lhs_lo[:, c, :], w_hi[:, c, :], start=False,
                                            stop=(c == KC - 1))
                return last

            def transposed(psum, src):
                for c in range(KC):
                    last = nc.tensor.transpose(psum[:, c * P:(c + 1) * P], src[:, c * P:(c + 1) * P],
                                               ident[:, :])
                return last

            def y_transpose(s, c):
                for t in range(BT):
                    last = nc.tensor.transpose(y_chunks[c][:, t * P:(t + 1) * P],
                                               y_in[:, s, t, c * P:(c + 1) * P], ident[:, :])
                last.then_inc(t_y, 1)

            def step(n, pair, p, slot, before, place, has):
                tail, head_of_tail, late_tail = not has(0), is_step(n, TILES), not has(0) and not is_step(n, TILES)
                if has(1):
                    need(pe, d_v, n - 1)
                    product(psum_v[:, :], xT_hi[:, 1 - p], xT_lo[:, 1 - p], WV, is_step(n, 1)).then_inc(t_v, 1)

                def attn_T():
                    pe.wait_ge(d_at, n - TB)
                    if not late_tail:
                        pe.wait_ge(a_qT, n - TB)
                    else:
                        pe.wait_ge(d_a, n - TB - 1)
                    transposed(psum_t, attn[:, :]).then_inc(t_a, 1)

                def q_T(lag):
                    pe.wait_ge(q_fetched[parity(p, lag)], 16 * pair - 16 * (TB // 2) + (
                        32 if p == 1 and lag == TB - 1 else 16))
                    if not tail:
                        if has(TB + 1):
                            pe.wait_ge(d_a, n - TB)
                    elif lag == TB:
                        pe.wait_ge(d_q, TILES)
                    else:
                        pe.wait_ge(a_qT, n - TB + 1)
                    transposed(psum_q if tail else psum_t, q_tile[:, parity(p, lag), :]).then_inc(t_qT, 1)

                def projection():
                    pe.wait_ge(d_a, n - TB)
                    need(pe, d_o, n - TB - 1)
                    if is_step(n, TB + 1):
                        pe.wait_ge(late_done, KC)
                    product(psum_o[:, :], aT_hi, aT_lo, WO).then_inc(t_o, 1)

                def numerators():
                    pe.wait_ge(a_qT, n - TB + 1)
                    if place == "first":
                        pe.wait_ge(a_kv, n)
                    need(pe, d_at, n - TB)
                    for c in range(NC):
                        last = nc.tensor.matmul(
                            psum_n[:, c // 2, (c % 2) * HC * EW:(c % 2 + 1) * HC * EW], qT_feat[:, c, :],
                            kv_diag[:, c].rearrange("p g e -> p (g e)"), start=True, stop=True)
                    last.then_inc(t_n, 1)

                def key_product():
                    need(pe, d_k, n)
                    product(psum_k[:, :], xT_hi[:, p], xT_lo[:, p], WK, is_step(n, 0)).then_inc(t_k, 1)

                if is_step(n, TB):
                    pe.wait_ge(ident_in, 16)
                if has(TB + 1):
                    attn_T()
                if late_tail:
                    if has(TB):
                        numerators()
                    if has(TB - 1):
                        q_T(TB - 1)
                    for c in y_chunk_in(n):
                        if c == 0:
                            pe.wait_ge(y_loaded[0], 16)
                        pe.wait_ge(y_chunks_free[c], TILES)
                        y_transpose(0, c)
                    if has(TB + 1):
                        projection()
                    return
                if head_of_tail:
                    q_T(TB)
                if has(0):
                    pe.wait_ge(d_x, n + 1)
                    need(pe, d_q, n)
                    product(psum_q[:, :], xT_hi[:, p], xT_lo[:, p], WQ, is_step(n, 0)).then_inc(t_q, 1)
                if has(TB + 1):
                    projection()
                if has(TB):
                    q_T(TB - 1 if head_of_tail else TB)
                k_first = x_ahead(has) or is_step(n, TB)
                if k_first:
                    key_product()
                if has(1):
                    pe.wait_ge(a_kf, n)
                    if place == "second":
                        need(pe, a_kv, n - 1)
                    for c in range(NC):
                        for g in range(HC):
                            h = c * HC + g
                            last = nc.tensor.matmul(
                                kv_cols[g * DH:(g + 1) * DH, c, :], k_feat[:, h * DH:(h + 1) * DH],
                                v_ext[:, h, :], start=(place == "second" and c == 0),
                                stop=(place == "first"), skip_group_check=True,
                                tile_position=(0, g * DH))
                    last.then_inc(t_kv, 1)
                if has(0) and not k_first:
                    key_product()
                if has(TB):
                    numerators()

            steps(pe, step)

            def mix_product(psum, lhs_hi, lhs_lo, rhs_hi, rhs_lo, ready=None):
                for c in range(KC):
                    if ready:
                        pe.wait_ge(*ready(c))
                    nc.tensor.matmul(psum, lhs_hi(c), rhs_hi(c), start=(c == 0), stop=False)
                    nc.tensor.matmul(psum, lhs_hi(c), rhs_lo(c), start=False, stop=False)
                    last = nc.tensor.matmul(psum, lhs_lo(c), rhs_hi(c), start=False, stop=(c == KC - 1))
                return last

            def mix_step(m, b, s, first):
                more = not (isinstance(m, int) and m == BLOCKS)
                if more and not first:
                    pe.wait_ge(y_loaded[s], 16 * b + 16)
                    for c in range(KC):
                        if c < 2:
                            pe.wait_ge(a_y, KC * m - KC + c + 1)
                        else:
                            pe.wait_ge(a_ru, KC * m - KC + c + 1)
                        y_transpose(s, c)
                if not first:
                    pe.wait_ge(d_ul, KC * m)
                    for t in range(BT):
                        need(pe, d_z, BT * m - BT + t - 1)
                        tok = slice(t * P, (t + 1) * P)
                        mix_product(psum_w[t % 2][:, :], lambda c: uT_hi[:, c, tok], lambda c: uT_lo[:, c, tok],
                                lambda c: wb_hi[:, WVF, c, :], lambda c: wb_lo[:, WVF, c, :]).then_inc(t_w, 1)
                if more:
                    for o in range(KC):
                        need(pe, a_ru, KC * m + o - 1)
                        feat = slice(o * P, (o + 1) * P)
                        mix_product(psum_u[o % 2][:, :], lambda c: wb_hi[:, WKF, c, feat],
                                lambda c: wb_lo[:, WKF, c, feat], lambda c: xk_hi[:, c, :],
                                lambda c: xk_lo[:, c, :],
                                (lambda c: (d_ml, 2 * KC * m + c + 1)) if o == 0 else None).then_inc(t_u, 1)
                    pe.wait_ge(d_ml, 2 * KC * m + 2 * KC)
                    for t in range(BT):
                        need(pe, a_g, BT * m + t - 1)
                        tok = slice(t * P, (t + 1) * P)
                        mix_product(psum_r[t % 2][:, :], lambda c: xr_hi[:, c, tok], lambda c: xr_lo[:, c, tok],
                                lambda c: wb_hi[:, WR, c, :], lambda c: wb_lo[:, WR, c, :]).then_inc(t_r, 1)

            blocks(pe, mix_step)

        @block.scalar
        def _(act):
            def late_high(chunks_of_step):
                for loaded, count, number, stage, hi, lo in chunks_of_step:
                    act.wait_ge(loaded, count)
                    nc.scalar.activation(hi, stage, ACT.Copy).then_inc(late_hi, 1)

            def chunks(psum):
                return psum[:, :].rearrange("p (c t) -> p c t", t=P)

            def chunks_high(w):
                for c in range(KC):
                    act.wait_ge(chunk_in[w][c], 16)
                    nc.scalar.activation(wa_hi[:, w, c], w_stage[w][:, c], ACT.Copy).then_inc(chunk_hi, 1)

            act.wait_ge(consts_set, 1)
            nc.scalar.activation(std_h[:, :], ln_eps[:, :], ACT.Sqrt)

            def y_copy(m, s, c):
                act.wait_ge(t_y, KC * m + c + 1)
                nc.scalar.activation(yT[:, s, c, 1:BLK + 1], y_chunks[c][:, :], ACT.Copy).then_inc(a_y, 1)

            def mix_high(m, i):
                act.wait_ge(d_m, 2 * KC * m + i + 1)
                nc.scalar.activation((xk_hi, xr_hi)[i // KC][:, i % KC, :], mix[:, i % 2, :], ACT.Copy) \
                    .then_inc(a_mh, 1)

            def step(n, pair, p, slot, before, place, has):
                tail, head_of_tail, late_tail = not has(0), is_step(n, TILES), not has(0) and not is_step(n, TILES)

                def q_feature(lag):
                    act.wait_ge(t_qT, n - lag + 1)
                    need(act, t_n, n - lag)
                    nc.scalar.activation(qT_feat[:, :, :], chunks(psum_q if tail else psum_t), ACT.Relu) \
                        .then_inc(a_qT, 1)

                def projection_rms(lag):
                    act.wait_ge(d_o, n - lag + 1)
                    if has(0):
                        act.wait_ge(a_sq, n + 1)
                    else:
                        act.wait_ge(a_so, n - lag)
                    nc.scalar.activation(squares[:, :], o_raw[:, :], ACT.Square,
                                         accum_out=sum_sq[:, 2:3]).then_inc(a_so, 1)
                    act.wait_ge(a_so, n - lag + 1)
                    nc.scalar.activation(sum_sq[:, 3:4], sum_sq[:, 2:3], ACT.Sqrt, bias=rms_eps[:, :],
                                         scale=1.0 / D).then_inc(a_ro, 1)

                if has(TB + 2) and not late_tail:
                    row = n * P - (TB + 2) * P
                    y_rows = y_mid[bass.ds(row if isinstance(row, int) else act.snap(row), P), :]

                def x_high(lead):
                    q = (p + lead) % 2
                    act.wait_ge(x_loaded[q], 16 * pair + (32 if lead and p else 16))
                    need(act, t_v, n + lead - 1)
                    nc.scalar.activation(xT_hi[:, q], xT_in[:, q], ACT.Copy).then_inc(a_x, 1)

                if has(0) and x_at_start(n, has):
                    x_high(0)
                if is_step(n, 0):
                    chunks_high(0)
                    chunks_high(1)
                    chunks_high(2)
                    x_high(1)
                if has(TB + 1):
                    act.wait_ge(t_a, n - TB)
                    need(act, t_o, n - TB - 1)
                    nc.scalar.activation(aT_hi[:, :, :], chunks(psum_t), ACT.Copy).then_inc(a_a, 1)
                if late_tail and has(TB + 2) and not is_step(n, TILES + 1):
                    projection_rms(TB + 2)
                if late_tail and has(TB - 1):
                    q_feature(TB - 1)
                for c in xk_chunk_in(n):
                    mix_high(0, c)
                for c in y_chunk_in(n):
                    if c == 0:
                        act.wait_ge(t_kv, TILES)
                    y_copy(0, 0, c)
                if has(1):
                    act.wait_ge(d_rk, n)
                    need(act, t_kv, n - 1)
                    nc.scalar.activation(v_ext[:, :, DH], ones[:, :], ACT.Copy, scale=inv_rms_k[:, :])
                    if x_ahead(has):
                        x_high(1)
                        if not is_step(n, 1):
                            late_high(late_chunks(n, p, pair)[0])
                    act.wait_ge(d_v, n)
                    nc.scalar.activation(v_ext[:, :, 0:DH], v_raw[:, :].rearrange("p (h d) -> p h d", d=DH),
                                         ACT.Copy, scale=inv_rms_k[:, :]).then_inc(a_v, 1)
                    act.wait_ge(g_kr, n)
                    nc.scalar.activation(k_feat[:, :], k_rot[:, :], ACT.Relu).then_inc(a_kf, 1)
                    if is_step(n, 1):
                        late_high(late_chunks(n, p, pair)[0])
                if has(TB + 2):
                    act.wait_ge(d_mv, n - TB - 1)
                    need(act, d_is, n - TB - 2)
                    nc.scalar.activation(std_h[:, :], mean_var[:, 1:2], ACT.Sqrt, bias=ln_eps[:, :]) \
                        .then_inc(a_std, 1)
                if has(0):
                    act.wait_ge(d_q, n + 1)
                    need(act, a_rms, n)
                    nc.scalar.activation(squares[:, :], q_raw[:, :], ACT.Square,
                                         accum_out=sum_sq[:, 0:1]).then_inc(a_sq, 1)
                if has(TB) and not late_tail:
                    q_feature(TB)
                    if place == "first":
                        act.wait_ge(t_kv, n)
                        for g in range(HC):
                            last = nc.scalar.activation(
                                kv_diag[g * DH:(g + 1) * DH, :, g, :], kv_cols[g * DH:(g + 1) * DH, :, :],
                                ACT.Copy)
                        last.then_inc(a_kv, TB)
                if has(TB + 1) and not late_tail:
                    projection_rms(TB + 1)
                if has(TB + 2) and not late_tail:
                    act.wait_ge(d_y, n - TB - 1)
                    act.dma_start(y_rows, y_out[:, p, :]).then_inc(y_stored[p], 16)
                if has(0):
                    act.wait_ge(d_k, n + 1)
                    act.wait_ge(a_sq, n + 1)
                    if has(TB + 1):
                        act.wait_ge(a_so, n - TB)
                    nc.scalar.activation(squares[:, :], k_raw[:, :], ACT.Square,
                                         accum_out=sum_sq[:, 1:2]).then_inc(a_sk, 1)
                    act.wait_ge(a_sk, n + 1)
                    need(act, d_rk, n)
                    nc.scalar.activation(rms_qk[:, :], sum_sq[:, 0:2], ACT.Sqrt, bias=rms_eps[:, :],
                                         scale=1.0 / D).then_inc(a_rms, 1)
                if head_of_tail:
                    q_feature(TB - 1)
                if has(1) and x_ahead(has):
                    late_high(late_chunks(n, p, pair)[1])

            steps(act, step)

            def mix_step(m, b, s, first):
                more = not (isinstance(m, int) and m == BLOCKS)
                if more:
                    need(act, d_m, 2 * KC * m - 2 * KC)
                    if s == 1:
                        act.wait_ge(a_y, KC * m)
                        nc.scalar.activation(yT[:, 1, :, 0], yT[:, 0, :, BLK], ACT.Copy).then_inc(a_c, 1)
                    if not first:
                        for c in range(KC):
                            y_copy(m, s, c)
                        for i in range(2 * KC):
                            if i == 0:
                                act.wait_ge(t_u, KC * m)
                            if i == KC:
                                act.wait_ge(t_r, BT * m)
                            mix_high(m, i)
                    need(act, t_w, BT * m)
                    for o in range(KC):
                        act.wait_ge(t_u, KC * m + o + 1)
                        need(act, g_u, KC * m + o - 1)
                        nc.scalar.activation(relu_u[:, o % 2, :], psum_u[o % 2][:, :], ACT.Relu) \
                            .then_inc(a_ru, 1)
                        act.wait_ge(a_ru, KC * m + o + 1)
                        nc.scalar.activation(uT_hi[:, o, :], relu_u[:, o % 2, :], ACT.Square).then_inc(a_uh, 1)
                        if first and o < 2:
                            mix_high(m, KC + 2 * o)
                            mix_high(m, KC + 2 * o + 1)
                if not first:
                    act.wait_ge(d_zm, BT * m)
                    nc.scalar.activation(z_std[:, :], z_mv[:, :, 1], ACT.Sqrt, bias=ln_eps[:, :]) \
                        .then_inc(a_zs, 1)
                if more:
                    need(act, d_z, BT * m)
                    for t in range(BT):
                        act.wait_ge(t_r, BT * m + t + 1)
                        nc.scalar.activation(gate[:, t, :], psum_r[t % 2][:, :], ACT.Sigmoid).then_inc(a_g, 1)

            blocks(act, mix_step)

        @block.vector
        def _(dve):
            def late_low(chunks_of_step):
                for loaded, count, number, stage, hi, lo in chunks_of_step:
                    dve.wait_ge(late_hi, number)
                    nc.vector.tensor_tensor(lo, stage, f32(hi), ALU.subtract).then_inc(late_done, 1)

            def chunks(psum):
                return psum[:, :].rearrange("p (c t) -> p c t", t=P)

            def times_cos(dst, src, slot):
                return nc.vector.tensor_tensor(
                    dst[:, :].rearrange("p (g f) -> p g f", f=HF), src[:, :].rearrange("p (g f) -> p g f", f=HF),
                    cos_t[:, slot, :].unsqueeze(1).to_broadcast([P, D // HF, HF]), ALU.mult)

            def times_sin(dst, src, slot):
                return nc.vector.tensor_tensor(
                    dst[:, :].rearrange("p (g f) -> p g f", f=DH), src[:, :].rearrange("p (g f) -> p g f", f=DH),
                    sin_t[:, slot, :].unsqueeze(1).to_broadcast([P, D // DH, DH]), ALU.mult)

            def chunks_low(w):
                for c in range(KC):
                    dve.wait_ge(chunk_hi, KC * w + c + 1)
                    nc.vector.tensor_tensor(wa_lo[:, w, c], w_stage[w][:, c], f32(wa_hi[:, w, c]),
                                            ALU.subtract).then_inc(chunk_done, 1)

            def mixed(m, s, i):
                c = i % KC
                if i < KC:
                    dve.wait_ge(g_d, KC * m + c + 1)
                if i >= 2:
                    dve.wait_ge(d_ml, 2 * KC * m + i - 1)
                nc.vector.scalar_tensor_tensor(
                    out=mix[:, i % 2, :], in0=diff[:, c, :], scalar=mu[:, 1 - i // KC, c:c + 1],
                    in1=yT[:, s, c, 0:BLK], op0=ALU.mult, op1=ALU.add).then_inc(d_m, 1)

            def low(m, i):
                dve.wait_ge(a_mh, 2 * KC * m + i + 1)
                nc.vector.tensor_tensor((xk_lo, xr_lo)[i // KC][:, i % KC, :], mix[:, i % 2, :],
                                        f32((xk_hi, xr_hi)[i // KC][:, i % KC, :]), ALU.subtract) \
                    .then_inc(d_ml, 1)

            def step(n, pair, p, slot, before, place, has):
                head_of_tail, late_tail = is_step(n, TILES), not has(0) and not is_step(n, TILES)

                def attention(lag):
                    dve.wait_ge(t_n, n - lag + 1)
                    nums = psum_n[:, :, 0:2 * HC * EW].rearrange("p b (h e) -> p b h e", e=EW)
                    den_v = den[:, :, :].rearrange("p s (b h) -> p s b h", b=2)
                    nc.vector.tensor_scalar(den_v[:, 0], nums[:, :, :, DH],
                                            eps_q[:, bass.ds(before if lag == TB + 1 else slot, 1)], None,
                                            ALU.add).then_inc(d_de, 1)
                    dve.wait_ge(d_de, n - lag + 1)
                    nc.vector.reciprocal(den[:, 1, :], den[:, 0, :]).then_inc(d_dr, 1)
                    dve.wait_ge(d_dr, n - lag + 1)
                    need(dve, t_a, n - lag)
                    for b in (0, 1):
                        last = nc.vector.tensor_tensor(
                            attn[:, b * D // 2:(b + 1) * D // 2].rearrange("p (h d) -> p h d", d=DH),
                            nums[:, b, :, 0:DH], den_v[:, 1, b].unsqueeze(2).to_broadcast([P, HEADS // 2, DH]),
                            ALU.mult)
                    last.then_inc(d_at, 1)

                def projection_norm(lag):
                    dve.wait_ge(a_ro, n - lag + 1)
                    nc.vector.reciprocal(inv_rms_o[:, :], sum_sq[:, 3:4]).then_inc(d_ro, 1)
                    dve.wait_ge(d_ro, n - lag + 1)
                    need(dve, g_h, n - lag)
                    nc.vector.scalar_tensor_tensor(out=h_sum[:, :], in0=o_raw[:, :], scalar=inv_rms_o[:, :],
                                                   in1=gain_o[:, :], op0=ALU.mult, op1=ALU.mult) \
                        .then_inc(d_on, 1)

                def k_read():
                    dve.wait_ge(t_k, n + 1)
                    need(dve, a_sk, n)
                    need(dve, g_kg, n)
                    nc.vector.tensor_tensor(k_raw[:, :], psum_k[:, :], bias_qkv[:, D:2 * D], ALU.add) \
                        .then_inc(d_k, 1)

                def projection_read():
                    dve.wait_ge(t_o, n - TB)
                    need(dve, a_so, n - TB - 1)
                    nc.vector.tensor_tensor(o_raw[:, :], psum_o[:, :], bias_o[:, :], ALU.add).then_inc(d_o, 1)

                if has(TB + 1) and not late_tail:
                    attention(TB + 1)
                def x_low(lead):
                    q = (p + lead) % 2
                    dve.wait_ge(a_x, n + lead + 1)
                    nc.vector.tensor_tensor(xT_lo[:, q], xT_in[:, q], f32(xT_hi[:, q]), ALU.subtract) \
                        .then_inc(d_x, 1)

                if has(0) and x_at_start(n, has):
                    x_low(0)
                if is_step(n, 0):
                    chunks_low(0)
                    chunks_low(1)
                    chunks_low(2)
                    x_low(1)
                    dve.wait_ge(bias_in, 16)
                if is_step(n, TB + 1):
                    for s in (0, 1):
                        dve.wait_ge(y_stored[s], 16)
                if has(1):
                    dve.wait_ge(a_rms, n)
                    need(dve, a_v, n - 1)
                    nc.vector.tensor_scalar(eps_q[:, bass.ds(before, 1)], rms_qk[:, 0:1], EPS_LIN, None, ALU.mult)
                    nc.vector.reciprocal(inv_rms_k[:, :], rms_qk[:, 1:2]).then_inc(d_rk, 1)
                    dve.wait_ge(g_kg, n)
                    need(dve, g_kr, n - 1)
                    times_cos(k_cos, k_g, before)
                    times_sin(k_sin, k_g, before).then_inc(d_kp, 1)
                    dve.wait_ge(t_v, n)
                    nc.vector.tensor_tensor(v_raw[:, :], psum_v[:, :], bias_qkv[:, 2 * D:3 * D], ALU.add) \
                        .then_inc(d_v, 1)
                if has(1) and x_ahead(has):
                    x_low(1)
                if has(TB + 1):
                    dve.wait_ge(a_a, n - TB)
                    nc.vector.tensor_tensor(aT_lo[:, :, :], chunks(psum_t), f32(aT_hi[:, :, :]), ALU.subtract) \
                        .then_inc(d_a, 1)
                for c in xk_chunk_in(n):
                    mixed(0, 0, c)
                if late_tail and has(TB + 2) and not is_step(n, TILES + 1):
                    projection_norm(TB + 2)
                if late_tail and has(TB):
                    attention(TB)
                for c in xk_chunk_in(n):
                    low(0, c)
                if has(TB + 2):
                    dve.wait_ge(g_h, n - TB - 1)
                    nc.vector.bn_stats(stats[:, :], h_sum[:, :]).then_inc(d_st, 1)
                    dve.wait_ge(consts_set, 1)
                    dve.wait_ge(d_st, n - TB - 1)
                    nc.vector.bn_aggr(mean_var[:, :], stats[:, :]).then_inc(d_mv, 1)
                if has(TB + 1) and late_tail:
                    projection_read()
                if has(0):
                    dve.wait_ge(t_q, n + 1)
                    need(dve, a_sq, n)
                    need(dve, g_qg, n)
                    nc.vector.tensor_tensor(q_raw[:, :], psum_q[:, :], bias_qkv[:, 0:D], ALU.add) \
                        .then_inc(d_q, 1)
                if has(1) and x_ahead(has):
                    late_low(late_chunks(n, p, pair)[0])
                if has(TB + 2):
                    dve.wait_ge(a_std, n - TB - 1)
                    nc.vector.reciprocal(inv_std[:, :], std_h[:, :]).then_inc(d_is, 1)
                    dve.wait_ge(d_is, n - TB - 1)
                    dve.wait_ge(y_stored[p], 16 * pair - 16 * (TB // 2))
                    nc.vector.tensor_scalar(y_out[:, p, :], h_sum[:, :], mean_var[:, 0:1], inv_std[:, :],
                                            ALU.subtract, ALU.mult).then_inc(d_y, 1)
                if is_step(n, 0):
                    k_read()
                if has(0):
                    dve.wait_ge(g_qg, n + 1)
                    if is_step(n, 0):
                        dve.wait_ge(const_in, 16 * CONSTS)
                    need(dve, g_qr, n)
                    times_cos(q_cos, q_g, slot)
                if has(TB + 1) and not late_tail:
                    projection_read()
                if has(0):
                    times_sin(q_sin, q_g, slot).then_inc(d_qp, 1)
                if has(TB + 1) and not late_tail:
                    projection_norm(TB + 1)
                if has(0) and not is_step(n, 0):
                    k_read()
                if head_of_tail:
                    attention(TB)
                if has(1) and x_ahead(has):
                    late_low(late_chunks(n, p, pair)[1])

            steps(dve, step)

            def tile_stats(m, t):
                dve.wait_ge(g_z, BT * m - BT + t + 1)
                nc.vector.bn_stats(z_stats[:, t, :], z[:, t, :]).then_inc(d_zs, 1)

            def mix_step(m, b, s, first):
                more = not (isinstance(m, int) and m == BLOCKS)

                for i in range(KC if first else 0, 2 * KC):
                    if more:
                        mixed(m, s, i)
                        if i > (KC if first else 0):
                            low(m, i - 1)
                    if not first and i % 2:
                        t = i // 2
                        dve.wait_ge(t_w, BT * m - BT + t + 1)
                        if t == 0:
                            dve.wait_ge(a_g, BT * m)
                            need(dve, d_zo, m - 1)
                        nc.vector.tensor_tensor(z[:, t, :], psum_w[t % 2][:, :], gate[:, t, :], ALU.mult) \
                            .then_inc(d_z, 1)
                        if not more and t:
                            tile_stats(m, t - 1)
                if more:
                    low(m, 2 * KC - 1)
                if not first:
                    for t in range(BT) if more else (BT - 1,):
                        tile_stats(m, t)
                    for t in range(BT):
                        dve.wait_ge(zero_set, 1)
                        dve.wait_ge(d_zs, BT * m - BT + t + 1)
                        nc.vector.bn_aggr(z_mv[:, t, :], z_stats[:, t, :]).then_inc(d_zm, 1)
                if more:
                    for o in range(KC):
                        dve.wait_ge(a_uh, KC * m + o + 1)
                        dve.wait_ge(g_u, KC * m + o + 1)
                        nc.vector.tensor_tensor(uT_lo[:, o, :], act_u[:, o % 2, :], f32(uT_hi[:, o, :]),
                                                ALU.subtract).then_inc(d_ul, 1)
                if not first:
                    dve.wait_ge(a_zs, m)
                    nc.vector.reciprocal(z_inv[:, :], z_std[:, :]).then_inc(d_zi, 1)
                    dve.wait_ge(d_zi, m)
                    if not (isinstance(m, int) and m == 1):
                        dve.wait_ge(out_stored, 16 * m - 16)
                    for t in range(BT):
                        last = nc.vector.tensor_scalar(z_out[:, t, :], z[:, t, :], z_mv[:, t, 0:1],
                                                       z_inv[:, t:t + 1], ALU.subtract, ALU.mult)
                    last.then_inc(d_zo, 1)

            blocks(dve, mix_step)

        @block.gpsimd
        def _(pool):
            pool.memset(rms_eps[:, :], RMS_EPS)
            pool.memset(ln_eps[:, :], LN_EPS)
            pool.memset(ones[:, :], 1.0)
            pool.memset(kv_diag[:, :, :, :], 0.0).then_inc(consts_set, 1)
            pool.wait_ge(const_in, 16 * CONSTS)
            pool.wait_ge(chunk_done, 2 * KC)

            def add_parts(dst, cos_part, sin_part):
                halves = [t.rearrange("p (h s f) -> p h s f", s=2, f=HF) for t in (dst, cos_part, sin_part)]
                for s in (0, 1):
                    last = nc.gpsimd.tensor_tensor(halves[0][:, :, s], halves[1][:, :, s],
                                                   halves[2][:, :, 1 - s], ALU.add)
                return last

            def difference(m, s, c):
                pool.wait_ge(a_y, KC * m + c + 1)
                nc.gpsimd.tensor_tensor(diff[:, c, :], yT[:, s, c, 1:BLK + 1], yT[:, s, c, 0:BLK],
                                        ALU.subtract).then_inc(g_d, 1)

            def step(n, pair, p, slot, before, place, has):
                def k_gained():
                    pool.wait_ge(d_k, n + 1)
                    need(pool, d_kp, n)
                    nc.gpsimd.tensor_tensor(k_g[:, :], k_raw[:, :], gain_qk[:, D:2 * D], ALU.mult).then_inc(g_kg, 1)

                if has(1):
                    pool.wait_ge(d_kp, n)
                    need(pool, a_kf, n - 1)
                    add_parts(k_rot[:, :], k_cos[:, :], k_sin[:, :]).then_inc(g_kr, 1)
                if has(0):
                    pool.wait_ge(d_q, n + 1)
                    need(pool, d_qp, n)
                    nc.gpsimd.tensor_tensor(q_g[:, :], q_raw[:, :], gain_qk[:, 0:D], ALU.mult).then_inc(g_qg, 1)
                    if is_step(n, 0):
                        k_gained()
                    pool.wait_ge(d_qp, n + 1)
                    if has(TB):
                        pool.wait_ge(q_fetched[p], 16 * pair - 16 * (TB // 2) + 16)
                    add_parts(q_ring[:, slot, :], q_cos[:, :], q_sin[:, :]).then_inc(g_qr, 1)
                for c in y_chunk_in(n):
                    if c == 0:
                        pool.wait_ge(t_kv, TILES)
                        pool.memset(yT[:, 0, :, 0:1], 0.0).then_inc(zero_set, 1)
                        pool.wait_ge(zero_set, 1)
                    difference(0, 0, c)
                if has(TB + 1):
                    pool.wait_ge(d_on, n - TB)
                    pool.wait_ge(res_loaded, 16 * n - 16 * TB)
                    need(pool, d_y, n - TB - 1)
                    nc.gpsimd.tensor_tensor(h_sum[:, :], h_sum[:, :], x_res[:, :], ALU.add).then_inc(g_h, 1)
                if has(0) and not is_step(n, 0):
                    k_gained()

            steps(pool, step)

            def mix_step(m, b, s, first):
                more = not (isinstance(m, int) and m == BLOCKS)
                if more:
                    need(pool, d_m, 2 * KC * m)
                    if s == 1:
                        pool.wait_ge(a_c, b + 1)
                    if not first:
                        for c in range(KC):
                            difference(m, s, c)
                if not first:
                    for t in range(BT):
                        pool.wait_ge(d_z, BT * m - BT + t + 1)
                        nc.gpsimd.tensor_tensor(z[:, t, :], z[:, t, :], y_in[:, 1 - s, t, :], ALU.add) \
                            .then_inc(g_z, 1)
                if more:
                    for o in range(KC):
                        pool.wait_ge(a_ru, KC * m + o + 1)
                        need(pool, d_ul, KC * m + o - 1)
                        nc.gpsimd.tensor_tensor(act_u[:, o % 2, :], relu_u[:, o % 2, :], relu_u[:, o % 2, :],
                                                ALU.mult).then_inc(g_u, 1)

            blocks(pool, mix_step)



def kernel(**inputs):
    import concourse.bacc as bacc
    from concourse.bass_utils import run_bass_kernel_spmd

    given = {name: np.asarray(a) for name, a in inputs.items()}
    x = given["L0_attn_x"]
    B, L, D = x.shape
    DH = D // HEADS
    order = np.arange(D).reshape(HEADS, DH // 2, 2).transpose(0, 2, 1).reshape(D)
    order_qkv = np.concatenate([order, D + order, 2 * D + np.arange(D)])
    exponents = np.arange(0, DH, 2, dtype=np.float32) / np.float32(DH)
    inv_freq = (1.0 / np.float32(10000.0) ** exponents).astype(np.float32)
    angles = np.outer(np.arange(L, dtype=np.float32), inv_freq).astype(np.float32)
    cos, sin = np.cos(angles), np.sin(angles)

    def laid(a):
        return np.ascontiguousarray(a)

    arrays = {
        "x": laid(x.reshape(B * L, D)),
        "x_T": laid(x.reshape(B * L // P, P, D // P, P).transpose(0, 3, 2, 1)),
        "w_qkv": laid(given["L0_attn_Wqkv"][order_qkv].T),
        "b_qkv": laid(given["L0_attn_bqkv"][order_qkv]),
        "g_qk": laid(np.concatenate([given["L0_attn_gq"][order], given["L0_attn_gk"][order]])),
        "w_out": laid(given["L0_attn_Wout"].T),
        "b_out": laid(given["L0_attn_bout"]),
        "g_out": laid(given["L0_attn_gout"]),
        "w_ffn": laid(np.concatenate([given[f"L0_ffn_W_{w}"].T for w in "rkv"])),
        "mu_r": laid(given["L0_ffn_mu_r"]),
        "mu_k": laid(given["L0_ffn_mu_k"]),
        "rope_cos": laid(cos),
        "rope_sin": laid(np.concatenate([sin, -sin], axis=1)),
        "identity": np.eye(P, dtype=np.float32),
    }
    nc = bacc.Bacc("TRN2", target_bir_lowering=False, num_devices=1, dynamic_dma_scratch_size=1024)
    args = {n: nc.dram_tensor(n, a.shape, mybir.dt.from_np(a.dtype), kind="ExternalInput").ap() for n, a in arrays.items()}
    out = nc.dram_tensor("out", (B * L, D), F32, kind="ExternalOutput").ap()
    y_mid = nc.dram_tensor("y_mid", (B * L, D), F32, kind="Internal").ap()
    postnorm_layer(nc, **args, out=out, y_mid=y_mid)
    r = run_bass_kernel_spmd(nc, [arrays], core_ids=[0])
    return r.results[0]["out"].reshape(B, L, D)
```
